# Optimizing a Trainium2 kernel written in Bass

```python
import numpy as np
import jax
import jax.numpy as jnp

def _softmax(x, axis=-1):
    return jax.nn.softmax(x, axis=axis)

def _gelu(x):
    return jax.nn.gelu(x, approximate=True)

def _silu(x):
    return jax.nn.silu(x)

def _sigmoid(x):
    return jax.nn.sigmoid(x)

def _layernorm(x, axis=-1, eps=1e-05):
    m = jnp.mean(x, axis=axis, keepdims=True)
    v = jnp.var(x, axis=axis, keepdims=True)
    return (x - m) / jnp.sqrt(v + eps)

def _scatter_add(tgt, idx, src, axis=0):
    return tgt.at[idx].add(src)

def _segment_sum(src, seg, n):
    return jax.ops.segment_sum(src, seg, n)
kernel_name = 'mk_vit_tower_d1_tok_img1024_r4_cdf952'

def setup_inputs(seed: int=0):
    np.random.seed(seed)
    _w = jnp.asarray

    def _rec_inputs():
        import jax
        import jax.numpy as jnp
        _rk = jax.random.key(seed)
        x = jax.random.uniform(jax.random.fold_in(_rk, 1), (16, 3, 256, 256), jnp.float32, 0.0, 1)
        return x
    x = _rec_inputs()

    def _L0_tok_setup():
        import jax, jax.numpy as jnp
        import numpy as np
        _GRAY_W = (0.2989, 0.587, 0.114)
        key = jax.random.key(seed)
        x = jax.random.uniform(key, (32, 3, 256, 256), dtype=jnp.float32)
        sx = jnp.array([[-3.0, 0.0, 3.0], [-10.0, 0.0, 10.0], [-3.0, 0.0, 3.0]], dtype=jnp.float32)
        scharr = jnp.stack([sx, sx.T])[:, None, :, :]
        return {'x': x, 'scharr': scharr}
    _L0_tok_all = _L0_tok_setup()
    _L0_tok_in = {k: v for k, v in _L0_tok_all.items() if k in ('scharr',)}
    del _L0_tok_all

    def _L0_attn_setup():
        import math
        import jax, jax.numpy as jnp
        import numpy as np
        D_MODEL = 256
        N_HEADS = 16
        D_K = D_MODEL // N_HEADS
        D_C = 64
        B, S = (2, 512)
        key = jax.random.key(seed)
        ks = jax.random.split(key, 7)
        sd = lambda fan_in: 1.0 / math.sqrt(fan_in)
        return {'x': jax.random.normal(ks[0], (B, S, D_MODEL), dtype=jnp.float32), 'W_dq': jax.random.uniform(ks[1], (D_MODEL, D_C), minval=-sd(D_MODEL), maxval=sd(D_MODEL), dtype=jnp.float32), 'W_uq': jax.random.uniform(ks[2], (D_C, N_HEADS * D_K), minval=-sd(D_C), maxval=sd(D_C), dtype=jnp.float32), 'W_dkv': jax.random.uniform(ks[3], (D_MODEL, D_C), minval=-sd(D_MODEL), maxval=sd(D_MODEL), dtype=jnp.float32), 'W_uk': jax.random.uniform(ks[4], (D_C, N_HEADS * D_K), minval=-sd(D_C), maxval=sd(D_C), dtype=jnp.float32), 'W_uv': jax.random.uniform(ks[5], (D_C, N_HEADS * D_K), minval=-sd(D_C), maxval=sd(D_C), dtype=jnp.float32), 'W_o': jax.random.uniform(ks[6], (N_HEADS * D_K, D_MODEL), minval=-sd(N_HEADS * D_K), maxval=sd(N_HEADS * D_K), dtype=jnp.float32)}
    _L0_attn_all = _L0_attn_setup()
    _L0_attn_in = {k: v for k, v in _L0_attn_all.items() if k in ('W_dq', 'W_uq', 'W_dkv', 'W_uk', 'W_uv', 'W_o')}
    del _L0_attn_all

    def _L0_ffn_setup():
        import jax, jax.numpy as jnp
        import numpy as np
        key = jax.random.key(seed)
        kx, kw = jax.random.split(key)
        x = jax.random.normal(kx, (32, 1024, 256), dtype=jnp.float32)
        weight = jax.random.normal(kw, (256, 256), dtype=jnp.float32) * 0.01
        return {'x': x, 'weight': weight}
    _L0_ffn_all = _L0_ffn_setup()
    _L0_ffn_in = {k: v for k, v in _L0_ffn_all.items() if k in ('weight',)}
    del _L0_ffn_all
    return {'x': x, 'L0_tok_scharr': _L0_tok_in['scharr'], 'L0_attn_W_dq': _L0_attn_in['W_dq'], 'L0_attn_W_uq': _L0_attn_in['W_uq'], 'L0_attn_W_dkv': _L0_attn_in['W_dkv'], 'L0_attn_W_uk': _L0_attn_in['W_uk'], 'L0_attn_W_uv': _L0_attn_in['W_uv'], 'L0_attn_W_o': _L0_attn_in['W_o'], 'L0_ffn_weight': _L0_ffn_in['weight']}

def reference(x, L0_tok_scharr, L0_attn_W_dq, L0_attn_W_uq, L0_attn_W_dkv, L0_attn_W_uk, L0_attn_W_uv, L0_attn_W_o, L0_ffn_weight):
    import jax
    import jax.numpy as jnp

    def _L0_tok_ref(x, scharr):
        import jax, jax.numpy as jnp
        import numpy as np
        _GRAY_W = (0.2989, 0.587, 0.114)
        w = jnp.asarray(_GRAY_W, dtype=x.dtype)
        gray = jnp.einsum('bchw,c->bhw', x, w)[:, None]
        edges = jax.lax.conv_general_dilated(gray, scharr, window_strides=(1, 1), padding='SAME', dimension_numbers=('NCHW', 'OIHW', 'NCHW'))
        abs_edges = jnp.sqrt(jnp.square(edges))
        edge = abs_edges.sum(axis=1) / 2
        return edge

    def _L0_attn_ref(x, W_dq, W_uq, W_dkv, W_uk, W_uv, W_o):
        import math
        import jax, jax.numpy as jnp
        import numpy as np
        D_MODEL = 256
        N_HEADS = 16
        D_K = D_MODEL // N_HEADS
        D_C = 64
        B, S = (2, 512)
        Bx, Sx, _ = x.shape
        c_q = x @ W_dq
        Q = (c_q @ W_uq).reshape(Bx, Sx, N_HEADS, D_K)
        c_kv = x @ W_dkv
        K = (c_kv @ W_uk).reshape(Bx, Sx, N_HEADS, D_K)
        V = (c_kv @ W_uv).reshape(Bx, Sx, N_HEADS, D_K)
        scores = jnp.einsum('bqhd,bkhd->bhqk', Q, K) / math.sqrt(D_K)
        causal = jnp.tril(jnp.ones((Sx, Sx), dtype=bool))
        scores = jnp.where(causal, scores, -jnp.inf)
        attn = jax.nn.softmax(scores, axis=-1)
        out = jnp.einsum('bhqk,bkhd->bqhd', attn, V).reshape(Bx, Sx, N_HEADS * D_K)
        return out @ W_o

    def _L0_ffn_ref(x, weight):
        import jax, jax.numpy as jnp
        import numpy as np
        b_weight = jnp.sign(weight)
        return jnp.einsum('bsi,oi->bso', x, b_weight)
    h = _L0_tok_ref(x, L0_tok_scharr)
    h = h + _L0_attn_ref(_layernorm(h, axis=-1), L0_attn_W_dq, L0_attn_W_uq, L0_attn_W_dkv, L0_attn_W_uk, L0_attn_W_uv, L0_attn_W_o)
    h = h + _L0_ffn_ref(_layernorm(h, axis=-1), L0_ffn_weight)
    return h

_drawn_inputs = setup_inputs


def setup_inputs(seed=0):
    import zlib

    import numpy as np

    out = dict(_drawn_inputs(seed))
    spreads = {}
    factors = {'L0_attn_W_dq': 8.0, 'L0_attn_W_uq': 8.0, 'L0_attn_W_uk': 8.0}
    for name, (base, spread) in spreads.items():
        noise = np.random.default_rng([zlib.crc32(name.encode()), seed]).standard_normal(out[name].shape)
        drawn = base * np.exp(spread * noise) if base else spread * noise
        out[name] = jnp.asarray(drawn.astype(out[name].dtype))
    for name, factor in factors.items():
        out[name] = (out[name] * factor).astype(out[name].dtype)
    return out
```

```python
import concourse.bass as bass
from concourse import mybir
from contextlib import ExitStack

F32 = mybir.dt.float32
BF16 = mybir.dt.bfloat16
ALU = mybir.AluOpType
ACT = mybir.ActivationFunctionType
AX = mybir.AxisListType

P = 128
IMAGES = 16
CH = 3
S = 256
D = 256
T = S // P
DC = 64
H = 16
DK = D // H
GRAY = (0.2989, 0.587, 0.114)
EPS = 1e-5

TAPS = 3
FILTERS = 2
RB = 32
NB = S // RB
RI = RB + TAPS - 1
KC = TAPS * RI
W2 = D + 2

PARTS = 3
Q_PARTS = (0, 0, 1, 0, 2, 1)
K_PARTS = (0, 1, 0, 2, 0, 1)
TERMS = len(Q_PARTS)
KQ = TERMS * DK
KM = KQ + PARTS
G = 4
NG = H // G
HALF = H // 2
VW = 32
MASK = -3.0e38
SCALE = DK ** -0.5


def build(nc, x, scharr, w_dq, w_uq, w_dkv, w_uk, w_uv, w_o, w_ffn, out):
    gray_dram = nc.dram_tensor("gray_padded", [IMAGES, S + 2, W2], F32, kind="Internal").ap()
    parts_dram = nc.dram_tensor("qk_parts", [IMAGES, 2 * PARTS, D, S], BF16, kind="Internal").ap()
    attn_dram = nc.dram_tensor("attn_scratch", [IMAGES, S, D], F32, kind="Internal").ap()

    with ExitStack() as whole:
        def keep(name, shape, dt):
            return whole.enter_context(nc.sbuf_tensor(name, shape, dt))

        ident = keep("ident", [P, P], F32)
        ident_bf = keep("ident_bf", [P, P], BF16)
        mask_bf = keep("mask_bf", [P, G, P], BF16)
        mask_kq = keep("mask_kq", [P, G, P], BF16)
        band = keep("band", [KC, FILTERS, RB], F32)
        w_c = keep("w_c", [P, T, 2 * DC], F32)
        w_q = keep("w_q", [P, D], F32)
        w_k = keep("w_k", [P, D], F32)
        w_v = keep("w_v", [P, D], F32)
        w_out = keep("w_out", [P, T, D], F32)
        w_sign = keep("w_sign", [P, T, D], F32)
        h_all = keep("h_all", [P, IMAGES, T, D], F32)
        v_all = keep("v_all", [P, IMAGES, T, H, VW], F32)

        constants(nc, scharr, w_dq, w_uq, w_dkv, w_uk, w_uv, w_o, w_ffn, gray_dram,
                  ident, ident_bf, mask_bf, mask_kq, band, w_c, w_q, w_k, w_v, w_out, w_sign, v_all)
        front(nc, x, gray_dram, parts_dram, ident, band, w_c, w_q, w_k, w_v, h_all, v_all)
        attention(nc, parts_dram, attn_dram, ident, ident_bf, mask_bf, mask_kq, v_all)
        tail(nc, attn_dram, out, ident, w_out, w_sign, h_all)


def held(count):
    return max(count, 0) if isinstance(count, int) else count


def steps(engine, step):
    for k in (-1, 0, 1, 2, 3):
        step(k // 2, k % 2)
    with engine.Fori(2, IMAGES // 2 - 1) as j:
        for u in range(2):
            step(j, u)
    for k in (IMAGES - 2, IMAGES - 1, IMAGES):
        step(k // 2, k % 2)


class At:

    def __init__(self, j, u, off):
        self.n = 2 * j + (u + off)
        self.slot = (u + off) % 2
        self.turn = j + ((u + off) // 2 + 1)
        self.live = not isinstance(self.n, int) or 0 <= self.n < IMAGES


def constants(nc, scharr, w_dq, w_uq, w_dkv, w_uk, w_uv, w_o, w_ffn, gray_dram,
              ident, ident_bf, mask_bf, mask_kq, band, w_c, w_q, w_k, w_v, w_out, w_sign, v_all):
    with ExitStack() as ctx:
        def sb(name, shape, dt):
            return ctx.enter_context(nc.sbuf_tensor(name, shape, dt))

        def sem(name):
            return ctx.enter_context(nc.semaphore(name))

        zeros = sb("zeros", [IMAGES, W2], F32)
        taps = sb("taps", [KC, FILTERS, TAPS], F32)
        diag = sb("diag", [KC, TAPS, RB], F32)
        w_raw = sb("w_raw", [P, T, D], F32)
        above = sb("above", [P, T, D], F32)
        below = sb("below", [P, T, D], F32)
        signs = sb("signs", [P, T, D], F32)
        ps_w = ctx.enter_context(nc.psum_tensor("ps_w", [P, T, D], F32))

        taps_in = sem("taps_in")
        ffn_in = sem("ffn_in")
        weights_in = sem("weights_in")
        zeroed = sem("zeroed")
        edges_out = sem("edges_out")
        cleared = sem("cleared")
        drawn = sem("drawn")
        band_step = sem("band_step")
        compared = sem("compared")
        signed = sem("signed")
        turned = sem("turned")
        sign_ready = sem("sign_ready")

        block = ctx.enter_context(nc.Block())

        @block.sync
        def _(sp):
            for dx in range(TAPS):
                src = bass.AP(scharr.tensor, scharr.offset + dx,
                              [[0, RI], [TAPS * TAPS, FILTERS], [TAPS, TAPS], [1, 1]])
                sp.dma_start(taps[dx * RI:(dx + 1) * RI, :, :].unsqueeze(3), src,
                             allow_slow_non_contiguous=True).then_inc(taps_in, 16)
            sp.dma_start(w_raw[:, :, :], w_ffn.rearrange("(t p) i -> p t i", p=P)).then_inc(ffn_in, 16)
            sp.dma_start(w_c[:, :, 0:DC], w_dq.rearrange("(t p) c -> p t c", p=P)).then_inc(weights_in, 16)
            sp.dma_start(w_c[:, :, DC:2 * DC], w_dkv.rearrange("(t p) c -> p t c", p=P)).then_inc(weights_in, 16)
            sp.dma_start(w_q[0:DC, :], w_uq).then_inc(weights_in, 16)
            sp.dma_start(w_k[DC:2 * DC, :], w_uk).then_inc(weights_in, 16)
            sp.dma_start(w_v[DC:2 * DC, :], w_uv).then_inc(weights_in, 16)
            sp.dma_start(w_out[:, :, :], w_o.rearrange("(t p) n -> p t n", p=P)).then_inc(weights_in, 16)
            sp.wait_ge(zeroed, 1)
            for row in (0, S + 1):
                sp.dma_start(gray_dram[:, row, :], zeros[:, :]).then_inc(edges_out, 16)
            sp.wait_ge(edges_out, 32)
            sp.wait_ge(weights_in, 6 * 16)

        @block.gpsimd
        def _(pool):
            pool.memset(zeros[:, :], 0.0).then_inc(zeroed, 1)
            pool.memset(ident[:, :], 0.0).then_inc(cleared, 1)
            pool.memset(ident_bf[:, :], 0.0).then_inc(cleared, 1)
            pool.memset(mask_bf[:, :, :], 0.0).then_inc(cleared, 1)
            pool.memset(mask_kq[:, :, :], 0.0).then_inc(cleared, 1)
            pool.memset(diag[:, :, :], 0.0).then_inc(cleared, 1)
            pool.wait_ge(cleared, 5)
            for m in (ident, ident_bf):
                pool.affine_select(out=m[:, :], in_=m[:, :], compare_op=ALU.not_equal, fill=1.0, base=0,
                                   pattern=[[-1, P]], channel_multiplier=1).then_inc(drawn, 1)
            pool.affine_select(out=mask_bf[:, :, :], in_=mask_bf[:, :, :], compare_op=ALU.is_ge, fill=MASK,
                               base=0, pattern=[[0, G], [-1, P]], channel_multiplier=1).then_inc(drawn, 1)
            pool.affine_select(out=mask_kq[:, :, :], in_=mask_kq[:, :, :], compare_op=ALU.is_ge, fill=MASK,
                               base=0, pattern=[[0, G], [1, P]], channel_multiplier=-1).then_inc(drawn, 1)
            for dx in range(TAPS):
                pool.wait_ge(drawn, 4 + dx)
                pool.affine_select(out=diag[:, :, :], in_=diag[:, :, :], compare_op=ALU.not_equal, fill=1.0,
                                   base=-dx * RI, pattern=[[-1, TAPS], [-1, RB]],
                                   channel_multiplier=1).then_inc(drawn, 1)

        @block.vector
        def _(dve):
            nc.vector.memset(v_all[:, :, :, :, DK:VW], 1.0)
            nc.vector.memset(w_q[DC:2 * DC, :], 0.0)
            nc.vector.memset(w_k[0:DC, :], 0.0)
            nc.vector.memset(w_v[0:DC, :], 0.0)
            dve.wait_ge(taps_in, 3 * 16)
            dve.wait_ge(drawn, 4 + TAPS)
            done = 0
            for f in range(FILTERS):
                nc.vector.tensor_scalar(band[:, f, :], diag[:, 0, :], taps[:, f, 0:1], None,
                                        ALU.mult).then_inc(band_step, 1)
                done += 1
                for dy in range(1, TAPS):
                    dve.wait_ge(band_step, done)
                    nc.vector.scalar_tensor_tensor(band[:, f, :], diag[:, dy, :], taps[:, f, dy:dy + 1],
                                                   band[:, f, :], ALU.mult, ALU.add).then_inc(band_step, 1)
                    done += 1
                dve.wait_ge(band_step, done)
                nc.vector.tensor_scalar(band[:, f, :], band[:, f, :], 0.5, None, ALU.mult)
            dve.wait_ge(ffn_in, 16)
            nc.vector.tensor_scalar(above[:, :, :], w_raw[:, :, :], 0.0, None, ALU.is_gt).then_inc(compared, 1)
            nc.vector.tensor_scalar(below[:, :, :], w_raw[:, :, :], 0.0, None, ALU.is_lt).then_inc(compared, 1)
            dve.wait_ge(compared, 2)
            nc.vector.tensor_tensor(signs[:, :, :], above[:, :, :], below[:, :, :],
                                    ALU.subtract).then_inc(signed, 1)
            dve.wait_ge(turned, 1)
            nc.vector.tensor_copy(w_sign[:, :, :], ps_w[:, :, :]).then_inc(sign_ready, 1)

        @block.tensor
        def _(pe):
            pe.wait_ge(drawn, 1)
            pe.wait_ge(signed, 1)
            for c in range(T):
                for t in range(T):
                    last = nc.tensor.transpose(ps_w[:, c, t * P:(t + 1) * P],
                                               signs[:, t, c * P:(c + 1) * P], ident[:, :])
            last.then_inc(turned, 1)

        @block.scalar
        def _(act):
            act.wait_ge(sign_ready, 1)


def front(nc, x, gray_dram, parts_dram, ident, band, w_c, w_q, w_k, w_v, h_all, v_all):
    with ExitStack() as ctx:
        def sb(name, shape, dt):
            return ctx.enter_context(nc.sbuf_tensor(name, shape, dt))

        def ps(name, shape, dt=F32):
            return ctx.enter_context(nc.psum_tensor(name, shape, dt))

        def sem(name):
            return ctx.enter_context(nc.semaphore(name))

        x_sb = sb("x_sb", [P, 2, CH, T, D], F32)
        gray = sb("gray", [P, 2, T, W2], F32)
        rows = sb("rows", [KC, 2, NB, D], F32)
        edge = sb("edge", [P, T, FILTERS, D], F32)
        stats = sb("stats", [P, T, 6], F32)
        mv = sb("mv", [P, T, 2], F32)
        var = sb("var", [P, T], F32)
        std = sb("std", [P, T], F32)
        rstd = sb("rstd", [P, T], F32)
        xn = sb("xn", [P, T, D], F32)
        xn_t = sb("xn_t", [P, T, S], F32)
        c_t = sb("c_t", [P, S], F32)
        qk_parts = sb("qk_parts_sb", [P, 2, 2, PARTS, T, S], BF16)
        rest = sb("rest", [P, 2, T, S], F32)

        ps_xt = ps("ps_xt", [P, T, S])
        ps_edge = ps("ps_edge", [P, T, FILTERS, D])
        ps_c = ps("ps_c", [P, 512])
        ps_qk = ps("ps_qk", [P, 2, T, S])
        ps_v = ps("ps_v", [P, T, D])

        x_in = [sem(f"x_in{i}") for i in range(2)]
        gray_out = [sem(f"gray_out{i}") for i in range(2)]
        rows_in = [sem(f"rows_in{i}") for i in range(2)]
        parts_out = [sem(f"parts_out{i}") for i in range(2)]
        bordered = sem("bordered")
        red_done = sem("red_done")
        green_done = sem("green_done")
        gray_done = sem("gray_done")
        edges_done = sem("edges_done")
        abs_done = sem("abs_done")
        h_done = sem("h_done")
        stats_done = sem("stats_done")
        mv_done = sem("mv_done")
        var_done = sem("var_done")
        std_done = sem("std_done")
        rstd_done = sem("rstd_done")
        passed = sem("passed")
        xn_done = sem("xn_done")
        xt_done = sem("xt_done")
        xt_copied = sem("xt_copied")
        c_done = sem("c_done")
        c_copied = sem("c_copied")
        qk_done = sem("qk_done")
        v_done = sem("v_done")
        v_copied = sem("v_copied")
        part1_done = sem("part1_done")
        rest_done = sem("rest_done")
        part2_done = sem("part2_done")
        part3_done = sem("part3_done")

        block = ctx.enter_context(nc.Block())

        @block.sync
        def _(sp):
            def load_x(a):
                sp.dma_start(x_sb[:, a.slot, :, :, :],
                             x[bass.ds(a.n, 1)].rearrange("a c (t p) w -> p (a c) t w", p=P)
                             ).then_inc(x_in[a.slot], 16)

            def step(j, u):
                load, here = At(j, u, 2), At(j, u, 1)
                if isinstance(here.n, int) and here.n == 0:
                    load_x(At(0, 0, 0))
                if load.live:
                    sp.wait_ge(gray_done, held(load.n - 1))
                    load_x(load)
                if here.live:
                    image = here.n * ((S + 2) * W2)
                    starts = [image + dx if isinstance(image, int) else sp.snap(image + dx)
                              for dx in range(TAPS)]
                    sp.wait_ge(gray_done, here.n + 1)
                    sp.sem_inc(passed)
                    sp.dma_start(gray_dram[bass.ds(here.n, 1), 1:S + 1, :]
                                 .rearrange("a (t p) w -> p (a t) w", p=P),
                                 gray[:, here.slot, :, :]).then_inc(gray_out[here.slot], 16)
                    sp.wait_ge(gray_out[here.slot], 16 * here.turn)
                    sp.sem_inc(passed)
                    sp.wait_ge(edges_done, held(T * (here.n - 1)))
                    sp.sem_inc(passed)
                    for dx in range(TAPS):
                        sp.dma_start(rows[dx * RI:(dx + 1) * RI, here.slot, :, :],
                                     bass.AP(gray_dram.tensor, starts[dx],
                                             [[W2, RI], [RB * W2, NB], [1, D]])
                                     ).then_inc(rows_in[here.slot], 16)

            steps(sp, step)

        @block.gpsimd
        def _(pool):
            pool.memset(gray[:, :, :, 0:1], 0.0)
            pool.memset(gray[:, :, :, W2 - 1:W2], 0.0).then_inc(bordered, 1)

            def step(j, u):
                done = At(j, u, -1)
                if done.live:
                    pool.wait_ge(part2_done, done.n + 1)
                    pool.tensor_tensor(qk_parts[:, done.slot, :, 2, :, :], rest[:, :, :, :],
                                       qk_parts[:, done.slot, :, 1, :, :], ALU.subtract).then_inc(part3_done, 1)
                    pool.wait_ge(part3_done, done.n + 1)
                    for i in range(2):
                        for t in range(T):
                            pool.dma_start(parts_dram[bass.ds(done.n, 1), i * PARTS:(i + 1) * PARTS,
                                                      t * P:(t + 1) * P, :].rearrange("a c p s -> p (a c) s"),
                                           qk_parts[:, done.slot, i, :, t, :]
                                           ).then_inc(parts_out[done.slot], 16)

            steps(pool, step)
            for s in range(2):
                pool.wait_ge(parts_out[s], 4 * 16 * IMAGES // 2)

        @block.scalar
        def _(act):
            act.wait_ge(bordered, 1)

            def step(j, u):
                ahead, here, done = At(j, u, 1), At(j, u, 0), At(j, u, -1)
                if ahead.live:
                    act.wait_ge(x_in[ahead.slot], 16 * ahead.turn)
                    act.wait_ge(gray_out[ahead.slot], held(16 * (ahead.turn - 1)))
                    nc.scalar.activation(gray[:, ahead.slot, :, 1:D + 1], x_sb[:, ahead.slot, 0, :, :],
                                         ACT.Copy, scale=GRAY[0]).then_inc(red_done, 1)
                if done.live:
                    act.wait_ge(xt_done, done.n + 1)
                    nc.scalar.copy(xn_t[:, :, :], ps_xt[:, :, :]).then_inc(xt_copied, 1)
                    act.wait_ge(c_done, done.n + 1)
                    nc.scalar.copy(c_t[:, :], ps_c[:, 0:S]).then_inc(c_copied, 1)
                if here.live:
                    for t in range(T):
                        act.wait_ge(edges_done, T * here.n + t + 1)
                        act.wait_ge(h_done, held(T * (here.n - 1) + t + 1))
                        nc.scalar.activation(edge[:, t, :, :], ps_edge[:, t, :, :], ACT.Abs).then_inc(abs_done, 1)
                if done.live:
                    act.wait_ge(qk_done, done.n + 1)
                    act.wait_ge(parts_out[done.slot], held(64 * (done.turn - 1)))
                    nc.scalar.copy(qk_parts[:, done.slot, :, 0, :, :], ps_qk[:, :, :, :]).then_inc(part1_done, 1)
                    act.wait_ge(v_done, done.n + 1)
                    nc.scalar.copy(v_all[:, bass.ds(done.n, 1), :, :, 0:DK]
                                   .rearrange("p a t h d -> p (a t) h d"),
                                   ps_v[:, :, :].rearrange("p t (h d) -> p t h d", h=H)).then_inc(v_copied, 1)
                if here.live:
                    act.wait_ge(var_done, here.n + 1)
                    nc.scalar.activation(std[:, :], var[:, :], ACT.Sqrt).then_inc(std_done, 1)

            steps(act, step)

        @block.vector
        def _(dve):
            def step(j, u):
                ahead, here, done = At(j, u, 1), At(j, u, 0), At(j, u, -1)
                if ahead.live:
                    g = gray[:, ahead.slot, :, 1:D + 1]
                    dve.wait_ge(red_done, ahead.n + 1)
                    nc.vector.scalar_tensor_tensor(g, x_sb[:, ahead.slot, 1, :, :], GRAY[1], g,
                                                   ALU.mult, ALU.add).then_inc(green_done, 1)
                    dve.wait_ge(green_done, ahead.n + 1)
                    nc.vector.scalar_tensor_tensor(g, x_sb[:, ahead.slot, 2, :, :], GRAY[2], g,
                                                   ALU.mult, ALU.add).then_inc(gray_done, 1)
                if here.live:
                    for t in range(T):
                        dve.wait_ge(abs_done, T * here.n + t + 1)
                        nc.vector.tensor_tensor(
                            h_all[:, bass.ds(here.n, 1), t, :].rearrange("p a d -> p (a d)"),
                            edge[:, t, 0, :], edge[:, t, 1, :], ALU.add).then_inc(h_done, 1)
                if done.live:
                    dve.wait_ge(part1_done, done.n + 1)
                    dve.wait_ge(part3_done, done.n)
                    nc.vector.tensor_tensor(rest[:, :, :, :], ps_qk[:, :, :, :],
                                            qk_parts[:, done.slot, :, 0, :, :], ALU.subtract).then_inc(rest_done, 1)
                if here.live:
                    for t in range(T):
                        dve.wait_ge(h_done, T * here.n + t + 1)
                        dve.sem_inc(passed)
                        nc.vector.bn_stats(stats[:, t, :], h_all[:, bass.ds(here.n, 1), t, :]
                                           .rearrange("p a d -> p (a d)")).then_inc(stats_done, 1)
                    for t in range(T):
                        dve.wait_ge(stats_done, T * here.n + t + 1)
                        dve.sem_inc(passed)
                        nc.vector.bn_aggr(mv[:, t, :], stats[:, t, :]).then_inc(mv_done, 1)
                    dve.wait_ge(mv_done, T * (here.n + 1))
                    nc.vector.tensor_scalar(var[:, :], mv[:, :, 1], EPS, None, ALU.add).then_inc(var_done, 1)
                if done.live:
                    dve.wait_ge(rest_done, done.n + 1)
                    nc.vector.tensor_copy(qk_parts[:, done.slot, :, 1, :, :], rest[:, :, :, :]
                                          ).then_inc(part2_done, 1)
                if here.live:
                    dve.wait_ge(std_done, here.n + 1)
                    nc.vector.reciprocal(rstd[:, :], std[:, :]).then_inc(rstd_done, 1)
                    dve.wait_ge(rstd_done, here.n + 1)
                    dve.wait_ge(xt_done, here.n)
                    for t in range(T):
                        nc.vector.tensor_scalar(xn[:, t, :], h_all[:, bass.ds(here.n, 1), t, :]
                                                .rearrange("p a d -> p (a d)"),
                                                mv[:, t, 0:1], rstd[:, t:t + 1],
                                                ALU.subtract, ALU.mult).then_inc(xn_done, 1)

            steps(dve, step)

        @block.tensor
        def _(pe):
            def filters(here, t):
                for f in range(FILTERS):
                    for b in range(P // RB):
                        last = nc.tensor.matmul(ps_edge[b * RB:(b + 1) * RB, t, f, :], band[:, f, :],
                                                rows[:, here.slot, t * (P // RB) + b, :],
                                                start=True, stop=True)
                last.then_inc(edges_done, 1)

            def step(j, u):
                here, done = At(j, u, 0), At(j, u, -1)
                if done.live:
                    pe.wait_ge(xn_done, T * (done.n + 1))
                    pe.wait_ge(xt_copied, held(done.n))
                    for c in range(T):
                        for t in range(T):
                            last = nc.tensor.transpose(ps_xt[:, c, t * P:(t + 1) * P],
                                                       xn[:, t, c * P:(c + 1) * P], ident[:, :])
                    last.then_inc(xt_done, 1)
                if here.live:
                    pe.wait_ge(rows_in[here.slot], 3 * 16 * here.turn)
                    pe.wait_ge(abs_done, held(T * here.n - 1))
                    filters(here, 0)
                if done.live:
                    pe.wait_ge(xt_copied, done.n + 1)
                    for c in range(T):
                        last = nc.tensor.matmul(ps_c[:, 0:S], w_c[:, c, :], xn_t[:, c, :],
                                                start=(c == 0), stop=(c == T - 1))
                    last.then_inc(c_done, 1)
                if here.live:
                    pe.wait_ge(abs_done, held(T * here.n))
                    filters(here, 1)
                if done.live:
                    pe.wait_ge(c_copied, done.n + 1)
                    pe.wait_ge(rest_done, held(done.n))
                    for i, w in enumerate((w_q, w_k)):
                        for t in range(T):
                            last = nc.tensor.matmul(ps_qk[:, i, t, :], w[:, t * P:(t + 1) * P], c_t[:, :],
                                                    start=True, stop=True)
                    last.then_inc(qk_done, 1)
                    pe.wait_ge(v_copied, held(done.n))
                    for t in range(T):
                        last = nc.tensor.matmul(ps_v[:, t, :], c_t[:, t * P:(t + 1) * P], w_v[:, :],
                                                start=True, stop=True)
                    last.then_inc(v_done, 1)

            steps(pe, step)


def attention(nc, parts_dram, attn_dram, ident, ident_bf, mask_bf, mask_kq, v_all):
    with ExitStack() as ctx:
        def sb(name, shape, dt):
            return ctx.enter_context(nc.sbuf_tensor(name, shape, dt))

        def ps(name, shape, dt=F32):
            return ctx.enter_context(nc.psum_tensor(name, shape, dt))

        def sem(name):
            return ctx.enter_context(nc.semaphore(name))

        q_st = sb("q_st", [P, 2, H, S], BF16)
        k_st = sb("k_st", [P, 2, H, S], BF16)
        v_now = sb("v_now", [P, 2, T, H, VW], F32)
        neg_max = sb("neg_max", [P, T, H], F32)
        max_rest = sb("max_rest", [P, 2, T, HALF], F32)
        max_parts = sb("max_parts", [P, T, PARTS, HALF], BF16)
        max_rows = sb("max_rows", [PARTS * HALF, S], BF16)
        probs = sb("probs", [P, NG, G, S + P], F32)
        o_un = sb("o_un", [P, 2, NG, S], F32)
        recip = sb("recip", [P, T, H], F32)
        attn = sb("attn", [P, T, D], F32)

        ps_hi = ps("ps_hi", [P, G, S])
        ps_lo = ps("ps_lo", [P, G, P])
        ps_k0 = ps("ps_k0", [P, G, S])
        ps_k1 = ps("ps_k1", [P, G, P])
        ps_o = ps("ps_o", [P, 512])
        ps_m = ps("ps_m", [P, 512])
        ps_mt = ps_m[:, :].bitcast(BF16)

        st_in = [[sem(f"st_in{s}{h}") for h in range(2)] for s in range(2)]
        v_in = [sem(f"v_in{s}") for s in range(2)]
        row_in = [sem(f"row_in{h}") for h in range(2)]
        ones_set = sem("ones_set")
        hi_done = sem("hi_done")
        lo_done = sem("lo_done")
        max_hi_done = sem("max_hi_done")
        max_lo_done = sem("max_lo_done")
        k0_done = sem("k0_done")
        k1_done = sem("k1_done")
        exp0_done = sem("exp0_done")
        exp1_done = sem("exp1_done")
        o_done = sem("o_done")
        o_copied = sem("o_copied")
        mp = [sem(f"max_part{i}") for i in range(5)]
        mt_done = sem("mt_done")
        mt_copied = sem("mt_copied")
        ot_done = sem("ot_done")
        recip_done = sem("recip_done")
        attn_done = sem("attn_done")
        attn_out = sem("attn_out")

        block = ctx.enter_context(nc.Block())

        @block.sync
        def _(sp):
            def load(a, hf):
                for st, parts, base in ((q_st, Q_PARTS, 0), (k_st, K_PARTS, PARTS)):
                    for term, part in enumerate(parts):
                        sp.dma_start(st[term * DK:(term + 1) * DK, a.slot, hf * HALF:(hf + 1) * HALF, :],
                                     parts_dram[bass.ds(a.n, 1), base + part,
                                                hf * HALF * DK:(hf + 1) * HALF * DK, :]
                                     .rearrange("a (h d) s -> d (a h) s", d=DK)).then_inc(st_in[a.slot][hf], 16)

            def rows_of_max(a, hf):
                sp.wait_ge(mt_copied, 2 * a.n + hf + 1)
                for part in range(PARTS):
                    sp.dma_start(q_st[KQ + part:KQ + part + 1, a.slot, hf * HALF:(hf + 1) * HALF, :],
                                 max_rows[part * HALF:(part + 1) * HALF, :]).then_inc(row_in[hf], 16)

            def step(j, u):
                ahead, here, done, past = At(j, u, 1), At(j, u, 0), At(j, u, -1), At(j, u, -2)
                if done.live:
                    rows_of_max(done, 1)
                if here.live:
                    sp.wait_ge(o_done, held(NG * (here.n - 1)))
                    sp.dma_start(v_now[:, here.slot, :, :, :].rearrange("p t h d -> p (t h d)"),
                                 v_all[:, bass.ds(here.n, 1), :, :, :].rearrange("p a t h d -> p (a t h d)")
                                 ).then_inc(v_in[here.slot], 16)
                if ahead.live:
                    sp.wait_ge(k1_done, held(NG * (ahead.n - 2) + 2))
                    load(ahead, 0)
                if here.live:
                    rows_of_max(here, 0)
                if past.live:
                    sp.wait_ge(attn_done, T * (past.n + 1))
                    sp.dma_start(attn_dram[bass.ds(past.n, 1)].rearrange("a (t p) d -> p (a t) d", p=P),
                                 attn[:, :, :]).then_inc(attn_out, 16)
                if ahead.live:
                    sp.wait_ge(k1_done, held(NG * (ahead.n - 1)))
                    load(ahead, 1)

            steps(sp, step)
            step(IMAGES // 2, 1)
            sp.wait_ge(attn_out, 16 * IMAGES)

        @block.gpsimd
        def _(pool):
            pool.memset(k_st[KQ:KM, :, :, :], 1.0).then_inc(ones_set, 1)


        @block.scalar
        def _(act):
            def copy_max_rows(a, hf):
                act.wait_ge(mt_done, 2 * a.n + hf + 1)
                if hf:
                    act.wait_ge(row_in[0], 48 * (a.n + 1))
                else:
                    act.wait_ge(row_in[1], held(48 * a.n))
                nc.scalar.copy(max_rows[:, :], ps_mt[0:PARTS * HALF, 0:S]).then_inc(mt_copied, 1)

            def step(j, u):
                here, done, past = At(j, u, 0), At(j, u, -1), At(j, u, -2)
                for g in range(NG):
                    if done.live:
                        at = NG * done.n + g
                        act.wait_ge(k0_done, at + 1)
                        act.wait_ge(o_done, held(at - NG + 1))
                        nc.scalar.activation(probs[:, g, :, 0:S], ps_k0[:, :, :], ACT.Exp,
                                             scale=SCALE).then_inc(exp0_done, 1)
                        act.wait_ge(k1_done, at + 1)
                        nc.scalar.activation(probs[:, g, :, S:S + P], ps_k1[:, :, :], ACT.Exp,
                                             scale=SCALE).then_inc(exp1_done, 1)
                    if g == 0 and done.live:
                        copy_max_rows(done, 1)
                    if g == 2 and here.live:
                        copy_max_rows(here, 0)
                    late = done if g >= 2 else past
                    if late.live:
                        lg = (g - 2) % NG
                        at = NG * late.n + lg
                        act.wait_ge(o_done, at + 1)
                        if lg == 0:
                            act.wait_ge(ot_done, held(T * (late.n - 1)))
                        nc.scalar.copy(o_un[:, late.slot, lg, :], ps_o[:, 0:S]).then_inc(o_copied, 1)

            steps(act, step)
            step(IMAGES // 2, 1)

        @block.vector
        def _(dve):
            def cut_max(a, hf):
                k = 2 * a.n + hf + 1
                heads = slice(hf * HALF, (hf + 1) * HALF)
                dve.wait_ge(max_hi_done, NG * a.n + 2 * hf + 2)
                dve.wait_ge(max_lo_done, NG * a.n + 2 * hf + 2)
                dve.wait_ge(mt_done, held(k - 1))
                nc.vector.tensor_copy(max_parts[:, :, 0, :], neg_max[:, :, heads]).then_inc(mp[0], 1)
                dve.wait_ge(mp[0], k)
                nc.vector.tensor_tensor(max_rest[:, 0, :, :], neg_max[:, :, heads], max_parts[:, :, 0, :],
                                        ALU.subtract).then_inc(mp[1], 1)
                dve.wait_ge(mp[1], k)
                nc.vector.tensor_copy(max_parts[:, :, 1, :], max_rest[:, 0, :, :]).then_inc(mp[2], 1)
                dve.wait_ge(mp[2], k)
                nc.vector.tensor_tensor(max_parts[:, :, 2, :], max_rest[:, 0, :, :], max_parts[:, :, 1, :],
                                        ALU.subtract).then_inc(mp[3], 1)

            def normalize(a, t):
                k = T * a.n + t + 1
                o = ps_m[:, :].rearrange("p (h d) -> p h d", d=VW)
                dve.wait_ge(ot_done, k)
                nc.vector.reciprocal(recip[:, t, :], o[:, :, DK]).then_inc(recip_done, 1)
                dve.wait_ge(recip_done, k)
                dve.wait_ge(attn_out, held(16 * a.n))
                nc.vector.tensor_tensor(attn[:, t, :].rearrange("p (h d) -> p h d", d=DK), o[:, :, 0:DK],
                                        recip[:, t, :].unsqueeze(2).to_broadcast([P, H, DK]),
                                        ALU.mult).then_inc(attn_done, 1)

            def step(j, u):
                here, past = At(j, u, 0), At(j, u, -2)
                for g in range(NG):
                    if here.live:
                        at = NG * here.n + g
                        heads = slice(g * G, (g + 1) * G)
                        dve.wait_ge(hi_done, at + 1)
                        nc.vector.tensor_reduce(neg_max[:, 1, heads], ps_hi[:, :, :], AX.X, ALU.max,
                                                negate=True).then_inc(max_hi_done, 1)
                        dve.wait_ge(lo_done, at + 1)
                        nc.vector.tensor_reduce(neg_max[:, 0, heads], ps_lo[:, :, :], AX.X, ALU.max,
                                                negate=True).then_inc(max_lo_done, 1)
                        if g % 2:
                            cut_max(here, g // 2)
                    if g == 2 and past.live:
                        normalize(past, 0)
                    if g == 3 and past.live:
                        normalize(past, 1)

            steps(dve, step)
            step(IMAGES // 2, 1)

        @block.tensor
        def _(pe):
            pe.wait_ge(ones_set, 1)
            two = G // 2

            def rows_scores(a, g):
                at = NG * a.n + g
                q = q_st[0:KQ, a.slot, :, :]
                k = k_st[0:KQ, a.slot, :, :]
                if g % 2 == 0:
                    pe.wait_ge(st_in[a.slot][g // 2], 16 * 2 * TERMS * a.turn)
                pe.wait_ge(max_hi_done, held(at))
                for b in range(2):
                    for i in range(two):
                        hh = g * G + b * two + i
                        nc.tensor.matmul(ps_hi[:, b * two + i, :], q[:, hh, P:S], k[:, hh, :],
                                         start=(i == 0), stop=False, skip_group_check=True)
                    last = nc.tensor.matmul(ps_hi[:, b * two:(b + 1) * two, P:S], ident_bf[:, :],
                                            mask_bf[:, 0:two, :], start=False, stop=True,
                                            skip_group_check=True)
                last.then_inc(hi_done, 1)
                pe.wait_ge(max_lo_done, held(at))
                for i in range(G):
                    hh = g * G + i
                    nc.tensor.matmul(ps_lo[:, i, :], q[:, hh, 0:P], k[:, hh, 0:P],
                                     start=(i == 0), stop=False, skip_group_check=True)
                nc.tensor.matmul(ps_lo[:, :, :], ident_bf[:, :], mask_bf[:, :, :], start=False, stop=True,
                                 skip_group_check=True).then_inc(lo_done, 1)

            def keys_scores(a, g):
                at = NG * a.n + g
                q = q_st[0:KM, a.slot, :, :]
                k = k_st[0:KM, a.slot, :, :]
                if g % 2 == 0:
                    pe.wait_ge(row_in[g // 2], 48 * (a.n + 1))
                pe.wait_ge(exp0_done, held(at))
                for b in range(2):
                    for i in range(two):
                        hh = g * G + b * two + i
                        nc.tensor.matmul(ps_k0[:, b * two + i, :], k[:, hh, 0:P], q[:, hh, :],
                                         start=(i == 0), stop=False, skip_group_check=True)
                    last = nc.tensor.matmul(ps_k0[:, b * two:(b + 1) * two, 0:P], ident_bf[:, :],
                                            mask_kq[:, 0:two, :], start=False, stop=True,
                                            skip_group_check=True)
                last.then_inc(k0_done, 1)
                pe.wait_ge(exp1_done, held(at))
                for i in range(G):
                    hh = g * G + i
                    nc.tensor.matmul(ps_k1[:, i, :], k[:, hh, P:S], q[:, hh, P:S],
                                     start=(i == 0), stop=False, skip_group_check=True)
                nc.tensor.matmul(ps_k1[:, :, :], ident_bf[:, :], mask_kq[:, :, :], start=False, stop=True,
                                 skip_group_check=True).then_inc(k1_done, 1)

            def values(a, g):
                at = NG * a.n + g
                if g == 0:
                    pe.wait_ge(v_in[a.slot], 16 * a.turn)
                pe.wait_ge(exp1_done, at + 1)
                pe.wait_ge(o_copied, held(at))
                for i in range(G):
                    nc.tensor.matmul(ps_o[i * VW:(i + 1) * VW, 0:S], v_now[:, a.slot, 0, g * G + i, :],
                                     probs[:, g, i, 0:S], start=True, stop=False, skip_group_check=True)
                for i in range(G):
                    last = nc.tensor.matmul(ps_o[i * VW:(i + 1) * VW, P:S], v_now[:, a.slot, 1, g * G + i, :],
                                            probs[:, g, i, S:S + P], start=False, stop=True,
                                            skip_group_check=True)
                last.then_inc(o_done, 1)

            def turn_max(a, hf):
                pe.wait_ge(mp[3], 2 * a.n + hf + 1)
                for t in range(T):
                    last = nc.tensor.transpose(ps_mt[0:PARTS * HALF, t * P:(t + 1) * P],
                                               max_parts[:, t, :, :].rearrange("p c h -> p (c h)"),
                                               ident_bf[:, :])
                last.then_inc(mt_done, 1)

            def turn_values(a, t):
                if t == 0:
                    pe.wait_ge(o_copied, NG * (a.n + 1))
                for g in range(NG):
                    last = nc.tensor.transpose(ps_m[:, g * P:(g + 1) * P], o_un[:, a.slot, g, t * P:(t + 1) * P],
                                               ident[:, :])
                last.then_inc(ot_done, 1)

            def step(j, u):
                here, done, past = At(j, u, 0), At(j, u, -1), At(j, u, -2)
                for g in range(NG):
                    if here.live:
                        rows_scores(here, g)
                    if g == 0 and done.live:
                        pe.wait_ge(mt_copied, 2 * done.n + 1)
                        pe.wait_ge(attn_done, held(T * (done.n - 1)))
                        turn_max(done, 1)
                    if g == 2 and here.live:
                        pe.wait_ge(mt_copied, held(2 * here.n))
                        turn_max(here, 0)
                    if done.live:
                        keys_scores(done, g)
                    late = done if g >= 2 else past
                    if late.live:
                        values(late, (g - 2) % NG)
                    if g == 2 and past.live:
                        if here.live:
                            pe.wait_ge(mt_copied, 2 * here.n + 1)
                        else:
                            pe.wait_ge(mt_copied, 2 * IMAGES)
                            pe.wait_ge(attn_done, T * past.n)
                        turn_values(past, 0)
                    if g == 3 and past.live:
                        pe.wait_ge(attn_done, T * past.n + 1)
                        turn_values(past, 1)

            steps(pe, step)
            step(IMAGES // 2, 1)


def tail(nc, attn_dram, out, ident, w_out, w_sign, h_all):
    with ExitStack() as ctx:
        def sb(name, shape, dt):
            return ctx.enter_context(nc.sbuf_tensor(name, shape, dt))

        def ps(name, shape, dt=F32):
            return ctx.enter_context(nc.psum_tensor(name, shape, dt))

        def sem(name):
            return ctx.enter_context(nc.semaphore(name))

        a_sb = sb("a_sb", [P, 2, T, D], F32)
        a_t = sb("a_t", [P, T, S], F32)
        y = sb("y", [P, 2, T, D], F32)
        stats = sb("stats2", [P, T, 6], F32)
        mv = sb("mv2", [P, T, 2], F32)
        var = sb("var2", [P, T], F32)
        std = sb("std2", [P, T], F32)
        rstd = sb("rstd2", [P, T], F32)
        yn = sb("yn", [P, T, D], F32)
        yn_t = sb("yn_t", [P, T, S], F32)
        z = sb("z", [P, 2, T, D], F32)

        ps_at = [ps(f"ps_at{s}", [P, T, S]) for s in range(2)]
        ps_y = [ps(f"ps_y{s}", [P, T, D]) for s in range(2)]
        ps_yt = [ps(f"ps_yt{s}", [P, T, S]) for s in range(2)]
        ps_z = [ps(f"ps_z{s}", [P, T, D]) for s in range(2)]

        a_in = [sem(f"a_in{s}") for s in range(2)]
        z_out = [sem(f"z_out{s}") for s in range(2)]
        at_done = sem("at_done")
        at_copied = sem("at_copied")
        proj_done = sem("proj_done")
        y_done = sem("y_done")
        stats_done = sem("stats2_done")
        mv_done = sem("mv2_done")
        var_done = sem("var2_done")
        std_done = sem("std2_done")
        rstd_done = sem("rstd2_done")
        passed = sem("passed2")
        yn_done = sem("yn_done")
        yt_done = sem("yt_done")
        yt_copied = sem("yt_copied")
        ffn_done = sem("ffn_done")
        z_done = sem("z_done")

        block = ctx.enter_context(nc.Block())

        @block.sync
        def _(sp):
            def step(j, u):
                ahead, done = At(j, u, 1), At(j, u, -1)
                if ahead.live:
                    sp.wait_ge(at_done, held(ahead.n - 1))
                    sp.dma_start(a_sb[:, ahead.slot, :, :],
                                 attn_dram[bass.ds(ahead.n, 1)].rearrange("a (t p) d -> p (a t) d", p=P)
                                 ).then_inc(a_in[ahead.slot], 16)
                if done.live:
                    sp.wait_ge(z_done, done.n + 1)
                    sp.dma_start(out[bass.ds(done.n, 1)].rearrange("a (t p) d -> p (a t) d", p=P),
                                 z[:, done.slot, :, :]).then_inc(z_out[done.slot], 16)

            steps(sp, step)
            for s in range(2):
                sp.wait_ge(z_out[s], 16 * IMAGES // 2)

        @block.scalar
        def _(act):
            def step(j, u):
                here, done = At(j, u, 0), At(j, u, -1)
                if here.live:
                    act.wait_ge(at_done, here.n + 1)
                    act.wait_ge(proj_done, held(here.n))
                    nc.scalar.copy(a_t[:, :, :], ps_at[here.slot][:, :, :]).then_inc(at_copied, 1)
                if done.live:
                    act.wait_ge(yt_done, done.n + 1)
                    act.wait_ge(ffn_done, held(done.n))
                    nc.scalar.copy(yn_t[:, :, :], ps_yt[done.slot][:, :, :]).then_inc(yt_copied, 1)
                if here.live:
                    act.wait_ge(var_done, here.n + 1)
                    nc.scalar.activation(std[:, :], var[:, :], ACT.Sqrt).then_inc(std_done, 1)

            steps(act, step)

        @block.vector
        def _(dve):
            def step(j, u):
                here, done = At(j, u, 0), At(j, u, -1)
                if here.live:
                    dve.wait_ge(proj_done, here.n + 1)
                    nc.vector.tensor_tensor(y[:, here.slot, :, :], ps_y[here.slot][:, :, :],
                                            h_all[:, bass.ds(here.n, 1), :, :]
                                            .rearrange("p a t d -> p (a t) d"), ALU.add).then_inc(y_done, 1)
                    dve.wait_ge(y_done, here.n + 1)
                    dve.sem_inc(passed)
                    for t in range(T):
                        nc.vector.bn_stats(stats[:, t, :], y[:, here.slot, t, :]).then_inc(stats_done, 1)
                    for t in range(T):
                        dve.wait_ge(stats_done, T * here.n + t + 1)
                        dve.sem_inc(passed)
                        nc.vector.bn_aggr(mv[:, t, :], stats[:, t, :]).then_inc(mv_done, 1)
                    dve.wait_ge(mv_done, T * (here.n + 1))
                    nc.vector.tensor_scalar(var[:, :], mv[:, :, 1], EPS, None, ALU.add).then_inc(var_done, 1)
                if done.live:
                    dve.wait_ge(ffn_done, done.n + 1)
                    dve.wait_ge(z_out[done.slot], held(16 * (done.turn - 1)))
                    nc.vector.tensor_tensor(z[:, done.slot, :, :], ps_z[done.slot][:, :, :],
                                            y[:, done.slot, :, :], ALU.add).then_inc(z_done, 1)
                if here.live:
                    dve.wait_ge(std_done, here.n + 1)
                    nc.vector.reciprocal(rstd[:, :], std[:, :]).then_inc(rstd_done, 1)
                    dve.wait_ge(rstd_done, here.n + 1)
                    dve.wait_ge(yt_done, held(here.n))
                    for t in range(T):
                        nc.vector.tensor_scalar(yn[:, t, :], y[:, here.slot, t, :],
                                                mv[:, t, 0:1], rstd[:, t:t + 1],
                                                ALU.subtract, ALU.mult).then_inc(yn_done, 1)

            steps(dve, step)

        @block.tensor
        def _(pe):
            def turn(dst, src, done):
                for c in range(T):
                    for t in range(T):
                        last = nc.tensor.transpose(dst[:, c, t * P:(t + 1) * P],
                                                   src[:, t, c * P:(c + 1) * P], ident[:, :])
                last.then_inc(done, 1)

            def product(dst, src_t, w, done):
                for t in range(T):
                    for c in range(T):
                        last = nc.tensor.matmul(dst[:, t, :], src_t[:, c, t * P:(t + 1) * P], w[:, c, :],
                                                start=(c == 0), stop=(c == T - 1))
                last.then_inc(done, 1)

            def step(j, u):
                here, done = At(j, u, 0), At(j, u, -1)
                if here.live:
                    pe.wait_ge(a_in[here.slot], 16 * here.turn)
                    pe.wait_ge(at_copied, held(here.n - 1))
                    turn(ps_at[here.slot], a_sb[:, here.slot, :, :], at_done)
                if done.live:
                    pe.wait_ge(yn_done, T * (done.n + 1))
                    pe.wait_ge(yt_copied, held(done.n - 1))
                    turn(ps_yt[done.slot], yn, yt_done)
                if here.live:
                    pe.wait_ge(at_copied, here.n + 1)
                    pe.wait_ge(y_done, held(here.n - 1))
                    product(ps_y[here.slot], a_t, w_out, proj_done)
                if done.live:
                    pe.wait_ge(yt_copied, done.n + 1)
                    pe.wait_ge(z_done, held(done.n - 1))
                    product(ps_z[done.slot], yn_t, w_sign, ffn_done)

            steps(pe, step)

        @block.gpsimd
        def _(pool):
            pool.wait_ge(z_done, IMAGES)


_INS = ['x', 'L0_tok_scharr', 'L0_attn_W_dq', 'L0_attn_W_uq', 'L0_attn_W_dkv', 'L0_attn_W_uk',
        'L0_attn_W_uv', 'L0_attn_W_o', 'L0_ffn_weight']


def kernel(**inputs):
    import numpy as _np
    import concourse.bacc as _bacc
    from concourse import mybir as _mybir
    from concourse.bass_utils import run_bass_kernel_spmd as _run

    nc = _bacc.Bacc("TRN2", target_bir_lowering=False, num_devices=1)
    arrays, args = {}, []
    for name in _INS:
        a = _np.ascontiguousarray(inputs[name])
        arrays[f"in_{name}"] = a
        args.append(nc.dram_tensor(f"in_{name}", a.shape, _mybir.dt.from_np(a.dtype), kind="ExternalInput").ap())
    out = nc.dram_tensor("out_dram", (IMAGES, S, D), F32, kind="ExternalOutput").ap()
    build(nc, *args, out)
    r = _run(nc, [arrays], core_ids=[0])
    return r.results[0]["out_dram"]
```

```python
import concourse.bass as bass
from concourse import mybir
from contextlib import ExitStack

F32 = mybir.dt.float32
BF16 = mybir.dt.bfloat16
ALU = mybir.AluOpType
ACT = mybir.ActivationFunctionType
AX = mybir.AxisListType

P = 128
IMAGES = 16
CH = 3
S = 256
D = 256
T = S // P
DC = 64
H = 16
DK = D // H
GRAY = (0.2989, 0.587, 0.114)
EPS = 1e-5

TAPS = 3
FILTERS = 2
RB = 32
NB = S // RB
RI = RB + TAPS - 1
KC = TAPS * RI
W2 = D + 2

PARTS = 3
SLOTS = 2 * PARTS
SLOTS_OF_PART = (slice(0, 5, 4), slice(1, 6, 4), slice(2, 4))
PRODUCTS = 6
FROM_Q = ((0, 0), (1, 0), (0, 2))
FROM_K = ((4, 1), (4, 1), (3, 1))
KQ = PRODUCTS * DK
KM = KQ + PARTS
G = 4
NG = H // G
HALF = H // T
VW = 32
MASK = -3.0e38
SCALE = DK ** -0.5


def held(count):
    return max(count, 0) if isinstance(count, int) else count


class At:

    def __init__(self, j, u, off):
        self.n = 2 * j + (u + off)
        self.slot = (u + off) % 2
        self.turn = j + ((u + off) // 2 + 1)
        self.live = not isinstance(self.n, int) or 0 <= self.n < IMAGES


def steps(engine, step, ahead, behind, first=None, last=None):
    first = -ahead if first is None else first
    last = IMAGES - 1 + behind if last is None else last
    lo = (behind + 3) // 2 * 2
    hi = (IMAGES - ahead) // 2 * 2
    for k in range(first, lo):
        step(k // 2, k % 2)
    if last >= hi:
        with engine.Fori(lo // 2, hi // 2) as j:
            for u in range(2):
                step(j, u)
    for k in range(hi, last + 1):
        step(k // 2, k % 2)


def build(nc, x, scharr, w_dq, w_uq, w_dkv, w_uk, w_uv, w_o, w_ffn, out):
    gray_dram = nc.dram_tensor("gray_padded", [IMAGES, S + 2, W2], F32, kind="Internal").ap()
    parts_dram = nc.dram_tensor("qk_parts", [IMAGES, SLOTS, T, P, S], BF16, kind="Internal").ap()
    attn_dram = nc.dram_tensor("attn_scratch", [IMAGES, S, D], F32, kind="Internal").ap()

    with ExitStack() as ctx:
        def sb(name, shape, dt=F32):
            return ctx.enter_context(nc.sbuf_tensor(name, shape, dt))

        def sem(name):
            return ctx.enter_context(nc.semaphore(name))

        ident = sb("ident", [P, P])
        ident_bf = sb("ident_bf", [P, P], BF16)
        mask_qk = sb("mask_qk", [P, G, P], BF16)
        mask_kq = sb("mask_kq", [P, 2, P], BF16)
        cap_kq = sb("cap_kq", [P, P])
        band = sb("band", [P, FILTERS, RB])
        w_c = sb("w_c", [P, T, 2 * DC])
        w_q = sb("w_q", [P, T, DK, HALF])
        w_k = sb("w_k", [P, T, DK, HALF])
        w_v = sb("w_v", [P, D])
        w_out = sb("w_out", [P, T, D])
        w_sign = sb("w_sign", [P, T, D])
        h_all = sb("h_all", [P, IMAGES, T, D])
        v_all = sb("v_all", [P, IMAGES, T, D])
        bank = ctx.enter_context(nc.psum_tensor("bank", [P, 8, 512], F32))

        shared = sb("shared", [P, 8192])
        x_sb = shared[:, 0:2 * CH * T * D].rearrange("p (s c t w) -> p s c t w", s=2, c=CH, t=T)
        rows = shared[:, 4096:8192].rearrange("p (s b w) -> p s b w", s=2, b=NB)
        gray = sb("gray", [P, 2, T, W2])
        edge = sb("edge", [P, T, FILTERS, D])
        stats = sb("stats", [P, T, 6])
        mv = sb("mv", [P, T, 2])
        var = sb("var", [P, T])
        std = sb("std", [P, T])
        rstd = sb("rstd", [P, T])
        xn = sb("xn", [P, T, D])
        xn_t = sb("xn_t", [P, T, S])
        c_t = sb("c_t", [P, 2, S])
        parts = sb("parts", [P, 2, SLOTS, T, S], BF16)
        rest = sb("rest", [P, 2, T, S])
        ps_xt = bank[:, 0, :].rearrange("p (c s) -> p c s", c=T)
        ps_edge = bank[:, 1:3, :].rearrange("p t (f w) -> p t f w", f=FILTERS)
        ps_c = bank[:, 3, 0:S]
        ps_qk = bank[:, 4:6, :].rearrange("p i (t s) -> p i t s", t=T)
        ps_v = bank[:, 6, :].rearrange("p (t d) -> p t d", t=T)

        q_st = sb("q_st", [P, 2, H, S], BF16)
        k_st = sb("k_st", [P, 2, H, S], BF16)
        v_now = sb("v_now", [P, 2, T, H, VW])
        neg_max = sb("neg_max", [P, T, H])
        max_rest = sb("max_rest", [P, T, HALF])
        max_parts = sb("max_parts", [P, T, PARTS, HALF], BF16)
        max_rows = sb("max_rows", [PARTS * HALF, S], BF16)
        probs = shared[:, 0:NG * G * (S + P)].rearrange("p (g h s) -> p g h s", g=NG, h=G)
        o_un = shared[:, NG * G * (S + P):].rearrange("p (s g q) -> p s g q", s=2, g=NG)
        recip = sb("recip", [P, T, H])
        attn = sb("attn", [P, T, D])
        ps_hi = bank[:, 0:2, :].rearrange("p b (h s) -> p (b h) s", s=S)
        ps_lo = bank[:, 2, :].rearrange("p (h s) -> p h s", s=P)
        ps_k0 = bank[:, 3:5, :].rearrange("p b (h s) -> p (b h) s", s=S)
        ps_k1 = bank[:, 5, :].rearrange("p (h s) -> p h s", s=P)
        ps_o = bank[:, 6, 0:S]
        ps_m = bank[:, 7, :]
        ps_mt = ps_m.bitcast(BF16)

        a_sb = sb("a_sb", [P, 2, T, D])
        a_t = sb("a_t", [P, T, S])
        y = parts[:, 0, :, :, :].rearrange("p c t s -> p (c t s)").bitcast(F32)[:, 0:2 * T * D] \
            .rearrange("p (s t d) -> p s t d", s=2, t=T)
        yn = xn
        yn_t = xn_t
        z = parts[:, 1, :, :, :].rearrange("p c t s -> p (c t s)").bitcast(F32)[:, 0:2 * T * D] \
            .rearrange("p (s t d) -> p s t d", s=2, t=T)
        ps_at = [bank[:, b, :].rearrange("p (c s) -> p c s", c=T) for b in (0, 1)]
        ps_y = [bank[:, b, :].rearrange("p (t d) -> p t d", t=T) for b in (2, 3)]
        ps_yt = [bank[:, b, :].rearrange("p (c s) -> p c s", c=T) for b in (4, 5)]
        ps_z = [bank[:, b, :].rearrange("p (t d) -> p t d", t=T) for b in (6, 7)]

        taps = neg_max[:, :, :].rearrange("p t h -> p (t h)")[:, 0:FILTERS * TAPS] \
            .rearrange("p (f y) -> p f y", f=FILTERS)
        diag = v_now[:, 0, 0, :, :].rearrange("p h d -> p (h d)")[:, 0:TAPS * RB] \
            .rearrange("p (y m) -> p y m", y=TAPS)
        zeros = v_now[:, 0, 1, :, :].rearrange("p h d -> p (h d)")[0:IMAGES, 0:W2]
        raw_q = v_now[:, 1, 0, :, :].rearrange("p h d -> p (h d)")[:, 0:D]
        raw_k = v_now[:, 1, 0, :, :].rearrange("p h d -> p (h d)")[:, D:2 * D]
        raw_w = a_sb[:, 0, :, :]
        above = a_sb[:, 1, :, :]
        signs = a_t
        ps_w = bank[:, 7, :].rearrange("p (c o) -> p c o", c=T)

        taps_in = sem("taps_in")
        ffn_in = sem("ffn_in")
        up_in = sem("up_in")
        weights_in = sem("weights_in")
        zeroed = sem("zeroed")
        edges_out = sem("edges_out")
        cleared = sem("cleared")
        drawn = sem("drawn")
        padded = sem("padded")
        band_step = sem("band_step")
        band_ready = sem("band_ready")
        compared = sem("compared")
        signed = sem("signed")
        turned = sem("turned")
        up_ready = sem("up_ready")
        sign_ready = sem("sign_ready")
        ones_set = sem("ones_set")
        passed = [sem(f"passed{i}") for i in range(3)]

        x_in = [sem(f"x_in{i}") for i in range(2)]
        gray_out = [sem(f"gray_out{i}") for i in range(2)]
        rows_in = [sem(f"rows_in{i}") for i in range(2)]
        parts_out = [sem(f"parts_out{i}") for i in range(2)]
        bordered = sem("bordered")
        red_done = sem("red_done")
        green_done = sem("green_done")
        gray_done = sem("gray_done")
        filters_done = sem("filters_done")
        abs_done = sem("abs_done")
        h_done = sem("h_done")
        stats_done = sem("stats_done")
        mv_done = sem("mv_done")
        var_done = sem("var_done")
        std_done = sem("std_done")
        rstd_done = sem("rstd_done")
        xn_done = sem("xn_done")
        xt_done = sem("xt_done")
        xt_copied = sem("xt_copied")
        c_done = sem("c_done")
        c_copied = sem("c_copied")
        qk_done = sem("qk_done")
        v_done = sem("v_done")
        v_copied = sem("v_copied")
        part0_done = sem("part0_done")
        rest_done = sem("rest_done")
        part1_done = sem("part1_done")
        part2_done = sem("part2_done")

        st_in = [[sem(f"st_in{s}{h}") for h in range(2)] for s in range(2)]
        v_ready = sem("v_ready")
        row_in = [sem(f"row_in{h}") for h in range(2)]
        hi_done = sem("hi_done")
        lo_done = sem("lo_done")
        max_hi_done = sem("max_hi_done")
        max_lo_done = sem("max_lo_done")
        k0_done = sem("k0_done")
        k1_done = sem("k1_done")
        capped = sem("capped")
        exp0_done = sem("exp0_done")
        exp1_done = sem("exp1_done")
        o_done = sem("o_done")
        o_copied = sem("o_copied")
        cut = [sem(f"cut{i}") for i in range(4)]
        mt_done = sem("mt_done")
        mt_copied = sem("mt_copied")
        ot_done = sem("ot_done")
        recip_done = sem("recip_done")
        attn_done = sem("attn_done")
        attn_out = sem("attn_out")

        a_in = [sem(f"a_in{s}") for s in range(2)]
        z_out = [sem(f"z_out{s}") for s in range(2)]
        at_done = sem("at_done")
        at_copied = sem("at_copied")
        proj_done = sem("proj_done")
        y_done = sem("y_done")
        stats2_done = sem("stats2_done")
        mv2_done = sem("mv2_done")
        var2_done = sem("var2_done")
        std2_done = sem("std2_done")
        rstd2_done = sem("rstd2_done")
        yn_done = sem("yn_done")
        yt_done = sem("yt_done")
        yt_copied = sem("yt_copied")
        ffn_done = sem("ffn_done")
        z_done = sem("z_done")

        block = ctx.enter_context(nc.Block())

        @block.sync
        def _(sp):
            def load_x(a):
                sp.dma_start(x_sb[:, a.slot, :, :, :],
                             x[bass.ds(a.n, 1)].rearrange("a c (t p) w -> p (a c) t w", p=P)
                             ).then_inc(x_in[a.slot], 16)

            def front(j, u):
                later, ahead, done = At(j, u, 4), At(j, u, 2), At(j, u, -3)
                first = isinstance(ahead.n, int) and ahead.n == 0
                if done.live:
                    sp.wait_ge(part2_done, done.n + 1)
                    sp.sem_inc(passed[0])
                    sp.dma_start(parts_dram[bass.ds(done.n, 1)].rearrange("a c t p s -> p (a c t) s"),
                                 parts[:, done.slot, :, :, :].rearrange("p c t s -> p (c t) s")
                                 ).then_inc(parts_out[done.slot], 16)
                if ahead.live:
                    image = ahead.n * ((S + 2) * W2)
                    starts = [image + dx if isinstance(image, int) else sp.snap(image + dx)
                              for dx in range(TAPS)]
                    sp.wait_ge(gray_done, ahead.n + 1)
                    sp.sem_inc(passed[0])
                    sp.dma_start(gray_dram[bass.ds(ahead.n, 1), 1:S + 1, :]
                                 .rearrange("a (t p) w -> p (a t) w", p=P),
                                 gray[:, ahead.slot, :, :]).then_inc(gray_out[ahead.slot], 16)
                    if later.live and not first:
                        load_x(later)
                    sp.wait_ge(filters_done, held(T * (ahead.n - 1)))
                    sp.sem_inc(passed[0])
                    sp.wait_ge(gray_out[ahead.slot], 16 * ahead.turn)
                    sp.sem_inc(passed[0])
                    if isinstance(ahead.n, int) and ahead.n < 2:
                        sp.wait_ge(edges_out, 32)
                        sp.wait_ge(padded, 3)
                    for dx in range(TAPS):
                        sp.dma_start(rows[dx * RI:(dx + 1) * RI, ahead.slot, :, :],
                                     bass.AP(gray_dram.tensor, starts[dx],
                                             [[W2, RI], [RB * W2, NB], [1, D]])
                                     ).then_inc(rows_in[ahead.slot], 16)
                if first:
                    load_x(later)

            block_of_slot = T * P * S

            def load_operands(a, hf):
                image = a.n * (SLOTS * block_of_slot)
                for st, pairs in ((q_st, FROM_Q), (k_st, FROM_K)):
                    for i, (first, stride) in enumerate(pairs):
                        start = image + (first * block_of_slot + hf * P * S)
                        start = start if isinstance(start, int) else sp.snap(start)
                        sp.dma_start(st[i * 2 * DK:(i + 1) * 2 * DK, a.slot, hf * HALF:(hf + 1) * HALF, :],
                                     bass.AP(parts_dram.tensor, start,
                                             [[stride * block_of_slot, 2], [HALF * S, DK], [1, HALF * S]])
                                     ).then_inc(st_in[a.slot][hf], 16)

            def rows_of_max(a, hf):
                sp.wait_ge(mt_copied, 2 * a.n + hf + 1)
                sp.sem_inc(passed[0])
                sp.dma_start(q_st[KQ:KM, a.slot, hf * HALF:(hf + 1) * HALF, :],
                             max_rows[:, :]).then_inc(row_in[hf], 16)

            def attention(j, u):
                ahead, here, done, past = At(j, u, 1), At(j, u, 0), At(j, u, -1), At(j, u, -2)
                if done.live:
                    rows_of_max(done, 1)
                if ahead.live and not (isinstance(ahead.n, int) and ahead.n < 1):
                    sp.wait_ge(k1_done, held(NG * (ahead.n - 2) + 2))
                    sp.sem_inc(passed[0])
                    load_operands(ahead, 0)
                if here.live:
                    rows_of_max(here, 0)
                if ahead.live and not (isinstance(ahead.n, int) and ahead.n < 1):
                    sp.wait_ge(k1_done, held(NG * (ahead.n - 1)))
                    sp.sem_inc(passed[0])
                    load_operands(ahead, 1)
                if past.live:
                    sp.wait_ge(attn_done, T * (past.n + 1))
                    sp.dma_start(attn_dram[bass.ds(past.n, 1)].rearrange("a (t p) d -> p (a t) d", p=P),
                                 attn[:, :, :]).then_inc(attn_out, 16)

            def tail(j, u):
                ahead, done = At(j, u, 2), At(j, u, -1)
                if ahead.live:
                    sp.wait_ge(at_done, held(ahead.n - 1))
                    if isinstance(ahead.n, int):
                        sp.wait_ge(attn_out, 16 * IMAGES if ahead.n >= 2 else 16 * (ahead.n + 3))
                    sp.dma_start(a_sb[:, ahead.slot, :, :],
                                 attn_dram[bass.ds(ahead.n, 1)].rearrange("a (t p) d -> p (a t) d", p=P)
                                 ).then_inc(a_in[ahead.slot], 16)
                if done.live:
                    sp.wait_ge(z_done, done.n + 1)
                    sp.dma_start(out[bass.ds(done.n, 1)].rearrange("a (t p) d -> p (a t) d", p=P),
                                 z[:, done.slot, :, :]).then_inc(z_out[done.slot], 16)

            LAST_X = IMAGES - 3

            load_x(At(0, 0, 0))
            load_x(At(0, 1, 0))
            sp.wait_ge(padded, 1)
            for dx in range(TAPS):
                sp.dma_start(taps[dx * RI:(dx + 1) * RI, :, :].unsqueeze(3),
                             bass.AP(scharr.tensor, scharr.offset + dx,
                                     [[0, RI], [TAPS * TAPS, FILTERS], [TAPS, TAPS], [1, 1]]),
                             allow_slow_non_contiguous=True).then_inc(taps_in, 16)
            sp.wait_ge(zeroed, 1)
            for row in (0, S + 1):
                sp.dma_start(gray_dram[:, row, :], zeros).then_inc(edges_out, 16)
            front(-1, 0)
            sp.dma_start(raw_q[0:DC, :], w_uq).then_inc(up_in, 16)
            sp.dma_start(raw_k[DC:2 * DC, :], w_uk).then_inc(up_in, 16)
            sp.dma_start(w_c[:, :, 0:DC], w_dq.rearrange("(t p) c -> p t c", p=P)).then_inc(weights_in, 16)
            sp.dma_start(w_c[:, :, DC:2 * DC], w_dkv.rearrange("(t p) c -> p t c", p=P)).then_inc(weights_in, 16)
            sp.dma_start(w_v[DC:2 * DC, :], w_uv).then_inc(weights_in, 16)
            sp.dma_start(raw_w, w_ffn.rearrange("(t p) i -> p t i", p=P)).then_inc(ffn_in, 16)
            sp.dma_start(w_out[:, :, :], w_o.rearrange("(t p) n -> p t n", p=P)).then_inc(weights_in, 16)
            steps(sp, front, 4, 3, first=-1, last=LAST_X)
            sp.wait_ge(parts_out[0], 16)
            load_operands(At(0, 0, 0), 0)
            load_operands(At(0, 0, 0), 1)
            for k in range(LAST_X + 1, IMAGES + 3):
                front(k // 2, k % 2)
            for s in range(2):
                sp.wait_ge(parts_out[s], 16 * IMAGES // 2)
            steps(sp, attention, 1, 2, first=0, last=IMAGES)
            for k in (-2, -1):
                tail(k // 2, k % 2)
            attention((IMAGES + 1) // 2, (IMAGES + 1) % 2)
            steps(sp, tail, 2, 1, first=0)
            sp.wait_ge(attn_out, 16 * IMAGES)
            for s in range(2):
                sp.wait_ge(z_out[s], 16 * IMAGES // 2)

        @block.gpsimd
        def _(pool):
            pool.memset(neg_max[:, :, :], 0.0).then_inc(padded, 1)
            for s in range(2):
                pool.wait_ge(padded, s + 1)
                pool.memset(rows[96:P, s, :, :], 0.0).then_inc(padded, 1)
            pool.wait_ge(padded, 3)
            pool.memset(v_now[:, 0, :, :, :], 0.0).then_inc(zeroed, 1)
            pool.memset(gray[:, :, :, 0:1], 0.0)
            pool.memset(gray[:, :, :, W2 - 1:W2], 0.0).then_inc(bordered, 1)
            pool.memset(ident[:, :], 0.0).then_inc(cleared, 1)
            pool.memset(ident_bf[:, :], 0.0).then_inc(cleared, 1)
            pool.memset(mask_qk[:, :, :], 0.0).then_inc(cleared, 1)
            pool.memset(mask_kq[:, :, :], 0.0).then_inc(cleared, 1)
            pool.memset(cap_kq[:, :], -MASK).then_inc(cleared, 1)
            pool.wait_ge(zeroed, 1)
            for dx in range(TAPS):
                if dx:
                    pool.wait_ge(drawn, dx)
                pool.affine_select(out=diag, in_=diag, compare_op=ALU.not_equal, fill=1.0,
                                   base=-dx * RI, pattern=[[-1, TAPS], [-1, RB]],
                                   channel_multiplier=1).then_inc(drawn, 1)
            pool.wait_ge(cleared, 5)
            for m in (ident, ident_bf):
                pool.affine_select(out=m[:, :], in_=m[:, :], compare_op=ALU.not_equal, fill=1.0, base=0,
                                   pattern=[[-1, P]], channel_multiplier=1).then_inc(drawn, 1)
            pool.affine_select(out=mask_qk[:, :, :], in_=mask_qk[:, :, :], compare_op=ALU.is_ge, fill=MASK,
                               base=0, pattern=[[0, G], [-1, P]], channel_multiplier=1).then_inc(drawn, 1)
            pool.affine_select(out=mask_kq[:, :, :], in_=mask_kq[:, :, :], compare_op=ALU.is_ge, fill=MASK,
                               base=0, pattern=[[0, 2], [1, P]], channel_multiplier=-1).then_inc(drawn, 1)
            pool.affine_select(out=cap_kq[:, :], in_=cap_kq[:, :], compare_op=ALU.is_ge, fill=MASK,
                               base=0, pattern=[[1, P]], channel_multiplier=-1).then_inc(drawn, 1)
            pool.wait_ge(drawn, TAPS + 5)
            pool.memset(k_st[KQ:KM, :, :, :], 1.0).then_inc(ones_set, 1)
            pool.wait_ge(ones_set, 1)

            def front(j, u):
                done = At(j, u, -2)
                if done.live:
                    pool.wait_ge(part1_done, done.n + 1)
                    pool.tensor_tensor(parts[:, done.slot, SLOTS_OF_PART[2], :, :], rest[:, :, :, :],
                                       parts[:, done.slot, SLOTS_OF_PART[1], :, :],
                                       ALU.subtract).then_inc(part2_done, 1)

            def cut_max(a, hf):
                k = 2 * a.n + hf + 1
                heads = slice(hf * HALF, (hf + 1) * HALF)
                pool.wait_ge(max_hi_done, NG * a.n + 2 * hf + 2)
                pool.wait_ge(max_lo_done, NG * a.n + 2 * hf + 2)
                pool.wait_ge(mt_done, held(k - 1))
                pool.sem_inc(passed[1])
                pool.tensor_copy(max_parts[:, :, 0, :], neg_max[:, :, heads]).then_inc(cut[0], 1)
                pool.wait_ge(cut[0], k)
                pool.tensor_tensor(max_rest[:, :, :], neg_max[:, :, heads], max_parts[:, :, 0, :],
                                   ALU.subtract).then_inc(cut[1], 1)
                pool.wait_ge(cut[1], k)
                pool.sem_inc(passed[1])
                pool.tensor_copy(max_parts[:, :, 1, :], max_rest[:, :, :]).then_inc(cut[2], 1)
                pool.wait_ge(cut[2], k)
                pool.tensor_tensor(max_parts[:, :, 2, :], max_rest[:, :, :], max_parts[:, :, 1, :],
                                   ALU.subtract).then_inc(cut[3], 1)

            def attention(j, u):
                here, done = At(j, u, 0), At(j, u, -1)
                if done.live:
                    cut_max(done, 1)
                if here.live:
                    cut_max(here, 0)
                    pool.wait_ge(o_done, held(NG * (here.n - 1)))
                    pool.sem_inc(passed[1])
                    for t in range(T):
                        last = pool.tensor_copy(v_now[:, here.slot, t, :, 0:DK],
                                                v_all[:, bass.ds(here.n, 1), t, :]
                                                .rearrange("p a (h d) -> p (a h) d", d=DK))
                    last.then_inc(v_ready, 1)

            steps(pool, front, 0, 2)
            pool.wait_ge(band_ready, 1)
            pool.wait_ge(up_ready, 1)
            pool.wait_ge(edges_out, 32)
            pool.memset(v_now[:, :, :, :, DK:VW], 1.0).then_inc(ones_set, 1)
            pool.wait_ge(v_copied, IMAGES)
            pool.wait_ge(ones_set, 2)
            steps(pool, attention, 0, 1)

        @block.scalar
        def _(act):
            def front(j, u):
                ahead, here, done, past = At(j, u, 2), At(j, u, 0), At(j, u, -1), At(j, u, -2)
                if ahead.live:
                    act.wait_ge(x_in[ahead.slot], 16 * ahead.turn)
                    act.wait_ge(gray_out[ahead.slot], held(16 * (ahead.turn - 1)))
                    nc.scalar.activation(gray[:, ahead.slot, :, 1:D + 1], x_sb[:, ahead.slot, 0, :, :],
                                         ACT.Copy, scale=GRAY[0]).then_inc(red_done, 1)
                if here.live:
                    for t in range(T):
                        act.wait_ge(filters_done, T * here.n + t + 1)
                        act.wait_ge(h_done, held(T * (here.n - 1) + t + 1))
                        nc.scalar.activation(edge[:, t, :, :], ps_edge[:, t, :, :], ACT.Abs).then_inc(abs_done, 1)
                if done.live:
                    act.wait_ge(xt_done, done.n + 1)
                    nc.scalar.copy(xn_t[:, :, :], ps_xt).then_inc(xt_copied, 1)
                if here.live:
                    act.wait_ge(var_done, here.n + 1)
                    nc.scalar.activation(std[:, :], var[:, :], ACT.Sqrt).then_inc(std_done, 1)
                if past.live:
                    act.wait_ge(qk_done, past.n + 1)
                    act.wait_ge(parts_out[past.slot], held(16 * (past.turn - 1)))
                    nc.scalar.copy(parts[:, past.slot, SLOTS_OF_PART[0], :, :], ps_qk[:, :, :, :]
                                   ).then_inc(part0_done, 1)
                if done.live:
                    act.wait_ge(c_done, done.n + 1)
                    act.wait_ge(v_done, held(done.n - 1))
                    nc.scalar.copy(c_t[:, done.slot, :], ps_c).then_inc(c_copied, 1)
                if past.live:
                    act.wait_ge(v_done, past.n + 1)
                    nc.scalar.copy(v_all[:, bass.ds(past.n, 1), :, :].rearrange("p a t d -> p (a t) d"),
                                   ps_v).then_inc(v_copied, 1)

            def copy_max_rows(a, hf):
                act.wait_ge(mt_done, 2 * a.n + hf + 1)
                if hf:
                    act.wait_ge(row_in[0], 16 * (a.n + 1))
                else:
                    act.wait_ge(row_in[1], held(16 * a.n))
                nc.scalar.copy(max_rows[:, :], ps_mt[0:PARTS * HALF, 0:S]).then_inc(mt_copied, 1)

            def attention(j, u):
                here, done, past = At(j, u, 0), At(j, u, -1), At(j, u, -2)
                for g in range(NG):
                    at = NG * done.n + g
                    if done.live:
                        act.wait_ge(k0_done, at + 1)
                        act.wait_ge(o_done, held(at - NG + 1))
                        nc.scalar.activation(probs[:, g, :, 0:S], ps_k0, ACT.Exp,
                                             scale=SCALE).then_inc(exp0_done, 1)
                    if g == 0 and done.live:
                        copy_max_rows(done, 1)
                    if g == 2 and here.live:
                        copy_max_rows(here, 0)
                    if done.live:
                        act.wait_ge(capped, at + 1)
                        nc.scalar.activation(probs[:, g, :, S:S + P], ps_k1, ACT.Exp,
                                             scale=SCALE).then_inc(exp1_done, 1)
                    late = done if g >= 2 else past
                    if late.live:
                        lg = (g - 2) % NG
                        act.wait_ge(o_done, NG * late.n + lg + 1)
                        if lg == 0:
                            act.wait_ge(ot_done, held(T * (late.n - 1)))
                        nc.scalar.copy(o_un[:, late.slot, lg, :], ps_o).then_inc(o_copied, 1)

            def tail(j, u):
                ahead, here, done = At(j, u, 1), At(j, u, 0), At(j, u, -1)
                if done.live:
                    act.wait_ge(yt_done, done.n + 1)
                    act.wait_ge(ffn_done, held(done.n))
                    nc.scalar.copy(yn_t[:, :, :], ps_yt[done.slot]).then_inc(yt_copied, 1)
                if ahead.live:
                    act.wait_ge(at_done, ahead.n + 1)
                    act.wait_ge(proj_done, held(ahead.n))
                    nc.scalar.copy(a_t[:, :, :], ps_at[ahead.slot]).then_inc(at_copied, 1)
                if here.live:
                    act.wait_ge(var2_done, here.n + 1)
                    nc.scalar.activation(std[:, :], var[:, :], ACT.Sqrt).then_inc(std2_done, 1)

            act.wait_ge(bordered, 1)
            steps(act, front, 2, 2)
            act.wait_ge(gray_done, IMAGES)
            act.wait_ge(filters_done, T * IMAGES)
            steps(act, attention, 0, 2)
            act.wait_ge(sign_ready, 1)
            steps(act, tail, 1, 1)

        @block.vector
        def _(dve):
            nc.vector.memset(raw_q[DC:2 * DC, :], 0.0)
            nc.vector.memset(raw_k[0:DC, :], 0.0)
            nc.vector.memset(w_v[0:DC, :], 0.0)

            def make_band():
                dve.wait_ge(taps_in, 3 * 16)
                dve.wait_ge(drawn, TAPS)
                done = 0
                for f in range(FILTERS):
                    nc.vector.tensor_scalar(band[:, f, :], diag[:, 0, :], taps[:, f, 0:1], None,
                                            ALU.mult).then_inc(band_step, 1)
                    done += 1
                    for dy in range(1, TAPS):
                        dve.wait_ge(band_step, done)
                        nc.vector.scalar_tensor_tensor(band[:, f, :], diag[:, dy, :], taps[:, f, dy:dy + 1],
                                                       band[:, f, :], ALU.mult, ALU.add).then_inc(band_step, 1)
                        done += 1
                dve.wait_ge(band_step, done)
                nc.vector.tensor_scalar(band[:, :, :], band[:, :, :], 0.5, None,
                                        ALU.mult).then_inc(band_ready, 1)

            def make_weights():
                dve.wait_ge(up_in, 2 * 16)
                for w, raw in ((w_q, raw_q), (w_k, raw_k)):
                    last = nc.vector.tensor_copy(w[:, :, :, :],
                                                 raw.rearrange("p (t h d) -> p t d h", t=T, d=DK))
                last.then_inc(up_ready, 1)
                dve.wait_ge(ffn_in, 16)
                nc.vector.tensor_scalar(above, raw_w, 0.0, None, ALU.is_gt).then_inc(compared, 1)
                dve.wait_ge(compared, 1)
                nc.vector.scalar_tensor_tensor(signs[:, :, :], raw_w, 0.0, above,
                                               ALU.is_lt, ALU.subtract).then_inc(compared, 1)
                dve.wait_ge(turned, 1)
                nc.vector.tensor_scalar(w_sign[:, :, :], ps_w, -1.0, None, ALU.mult).then_inc(sign_ready, 1)

            def front(j, u):
                ahead, here, past = At(j, u, 2), At(j, u, 0), At(j, u, -2)
                if ahead.live:
                    g = gray[:, ahead.slot, :, 1:D + 1]
                    dve.wait_ge(red_done, ahead.n + 1)
                    nc.vector.scalar_tensor_tensor(g, x_sb[:, ahead.slot, 1, :, :], GRAY[1], g,
                                                   ALU.mult, ALU.add).then_inc(green_done, 1)
                    dve.wait_ge(green_done, ahead.n + 1)
                    nc.vector.scalar_tensor_tensor(g, x_sb[:, ahead.slot, 2, :, :], GRAY[2], g,
                                                   ALU.mult, ALU.add).then_inc(gray_done, 1)
                if here.live:
                    for t in range(T):
                        dve.wait_ge(abs_done, T * here.n + t + 1)
                        nc.vector.tensor_tensor(
                            h_all[:, bass.ds(here.n, 1), t, :].rearrange("p a d -> p (a d)"),
                            edge[:, t, 0, :], edge[:, t, 1, :], ALU.add).then_inc(h_done, 1)
                    for t in range(T):
                        dve.wait_ge(h_done, T * here.n + t + 1)
                        dve.sem_inc(passed[2])
                        nc.vector.bn_stats(stats[:, t, :], h_all[:, bass.ds(here.n, 1), t, :]
                                           .rearrange("p a d -> p (a d)")).then_inc(stats_done, 1)
                    for t in range(T):
                        dve.wait_ge(stats_done, T * here.n + t + 1)
                        dve.sem_inc(passed[2])
                        nc.vector.bn_aggr(mv[:, t, :], stats[:, t, :]).then_inc(mv_done, 1)
                    dve.wait_ge(mv_done, T * (here.n + 1))
                    nc.vector.tensor_scalar(var[:, :], mv[:, :, 1], EPS, None, ALU.add).then_inc(var_done, 1)
                if here.live:
                    dve.wait_ge(std_done, here.n + 1)
                    nc.vector.reciprocal(rstd[:, :], std[:, :]).then_inc(rstd_done, 1)
                    dve.wait_ge(rstd_done, here.n + 1)
                    dve.wait_ge(xt_done, held(here.n))
                    for t in range(T):
                        nc.vector.tensor_scalar(xn[:, t, :], h_all[:, bass.ds(here.n, 1), t, :]
                                                .rearrange("p a d -> p (a d)"),
                                                mv[:, t, 0:1], rstd[:, t:t + 1],
                                                ALU.subtract, ALU.mult).then_inc(xn_done, 1)
                if past.live:
                    p0, p1 = (parts[:, past.slot, s, :, :] for s in SLOTS_OF_PART[:2])
                    dve.wait_ge(part0_done, past.n + 1)
                    dve.wait_ge(part2_done, held(past.n))
                    nc.vector.tensor_tensor(rest[:, :, :, :], ps_qk[:, :, :, :], p0,
                                            ALU.subtract).then_inc(rest_done, 1)
                    dve.wait_ge(rest_done, past.n + 1)
                    nc.vector.tensor_copy(p1, rest[:, :, :, :]).then_inc(part1_done, 1)

            def normalize(a, t):
                k = T * a.n + t + 1
                o = ps_m.rearrange("p (h d) -> p h d", d=VW)
                dve.wait_ge(ot_done, k)
                nc.vector.reciprocal(recip[:, t, :], o[:, :, DK]).then_inc(recip_done, 1)
                dve.wait_ge(recip_done, k)
                dve.wait_ge(attn_out, held(16 * a.n))
                nc.vector.tensor_tensor(attn[:, t, :].rearrange("p (h d) -> p h d", d=DK), o[:, :, 0:DK],
                                        recip[:, t, :].unsqueeze(2).to_broadcast([P, H, DK]),
                                        ALU.mult).then_inc(attn_done, 1)

            def attention(j, u):
                here, done, past = At(j, u, 0), At(j, u, -1), At(j, u, -2)
                for g in range(NG):
                    at = NG * here.n + g
                    heads = slice(g * G, (g + 1) * G)
                    if g == 3 and past.live:
                        normalize(past, 0)
                    if here.live:
                        if g % 2 == 0:
                            dve.wait_ge(cut[1], held(2 * here.n - 1 + g // 2))
                        dve.wait_ge(hi_done, at + 1)
                        nc.vector.tensor_reduce(neg_max[:, 1, heads], ps_hi, AX.X, ALU.max,
                                                negate=True).then_inc(max_hi_done, 1)
                    if here.live:
                        dve.wait_ge(lo_done, at + 1)
                        nc.vector.tensor_reduce(neg_max[:, 0, heads], ps_lo, AX.X, ALU.max,
                                                negate=True).then_inc(max_lo_done, 1)
                    if done.live:
                        dve.wait_ge(k1_done, NG * done.n + g + 1)
                        nc.vector.tensor_tensor(ps_k1, ps_k1,
                                                cap_kq[:, :].unsqueeze(1).to_broadcast([P, G, P]),
                                                ALU.min).then_inc(capped, 1)
                    if g == 3 and past.live:
                        normalize(past, 1)

            def tail(j, u):
                here, done = At(j, u, 0), At(j, u, -1)
                if here.live:
                    dve.wait_ge(proj_done, here.n + 1)
                    dve.wait_ge(z_done, held(here.n - 1))
                    nc.vector.tensor_tensor(y[:, here.slot, :, :], ps_y[here.slot],
                                            h_all[:, bass.ds(here.n, 1), :, :]
                                            .rearrange("p a t d -> p (a t) d"), ALU.add).then_inc(y_done, 1)
                    dve.wait_ge(y_done, here.n + 1)
                    dve.sem_inc(passed[2])
                    for t in range(T):
                        nc.vector.bn_stats(stats[:, t, :], y[:, here.slot, t, :]).then_inc(stats2_done, 1)
                    for t in range(T):
                        dve.wait_ge(stats2_done, T * here.n + t + 1)
                        dve.sem_inc(passed[2])
                        nc.vector.bn_aggr(mv[:, t, :], stats[:, t, :]).then_inc(mv2_done, 1)
                    dve.wait_ge(mv2_done, T * (here.n + 1))
                    nc.vector.tensor_scalar(var[:, :], mv[:, :, 1], EPS, None, ALU.add).then_inc(var2_done, 1)
                    dve.wait_ge(std2_done, here.n + 1)
                    nc.vector.reciprocal(rstd[:, :], std[:, :]).then_inc(rstd2_done, 1)
                    dve.wait_ge(rstd2_done, here.n + 1)
                    dve.wait_ge(yt_done, held(here.n))
                    for t in range(T):
                        nc.vector.tensor_scalar(yn[:, t, :], y[:, here.slot, t, :],
                                                mv[:, t, 0:1], rstd[:, t:t + 1],
                                                ALU.subtract, ALU.mult).then_inc(yn_done, 1)
                if done.live:
                    dve.wait_ge(ffn_done, done.n + 1)
                    dve.wait_ge(z_out[done.slot], held(16 * (done.turn - 1)))
                    nc.vector.tensor_tensor(z[:, done.slot, :, :], ps_z[done.slot],
                                            y[:, done.slot, :, :], ALU.add).then_inc(z_done, 1)

            def front_step(j, u):
                front(j, u)
                if isinstance(j, int) and 2 * j + u == -2:
                    make_band()
                if isinstance(j, int) and 2 * j + u == -1:
                    make_weights()

            steps(dve, front_step, 2, 2)
            dve.wait_ge(drawn, TAPS + 5)
            steps(dve, attention, 0, 2)
            steps(dve, tail, 0, 1)

        @block.tensor
        def _(pe):
            def turn(dst, src, done):
                for c in range(T):
                    for t in range(T):
                        last = nc.tensor.transpose(dst[:, c, t * P:(t + 1) * P],
                                                   src[:, t, c * P:(c + 1) * P], ident[:, :])
                last.then_inc(done, 1)

            def filters(here, t):
                for f in range(FILTERS):
                    for b in range(P // RB):
                        last = nc.tensor.matmul(ps_edge[b * RB:(b + 1) * RB, t, f, :], band[:, f, :],
                                                rows[:, here.slot, t * (P // RB) + b, :],
                                                start=True, stop=True)
                last.then_inc(filters_done, 1)

            def front(j, u):
                here, done, past = At(j, u, 0), At(j, u, -1), At(j, u, -2)
                if here.live:
                    pe.wait_ge(rows_in[here.slot], 3 * 16 * here.turn)
                    for t in range(T):
                        pe.wait_ge(abs_done, held(T * (here.n - 1) + t + 1))
                        filters(here, t)
                if done.live:
                    pe.wait_ge(xn_done, T * (done.n + 1))
                    pe.wait_ge(xt_copied, held(done.n))
                    turn(ps_xt, xn, xt_done)
                if past.live:
                    pe.wait_ge(c_copied, past.n + 1)
                    pe.wait_ge(rest_done, held(past.n))
                    for i, w in enumerate((w_q, w_k)):
                        for t in range(T):
                            last = nc.tensor.matmul(ps_qk[:, i, t, :],
                                                    w[:, t, :, :].rearrange("p d h -> p (d h)"),
                                                    c_t[:, past.slot, :], start=True, stop=True)
                    last.then_inc(qk_done, 1)
                if done.live:
                    pe.wait_ge(xt_copied, done.n + 1)
                    for c in range(T):
                        last = nc.tensor.matmul(ps_c, w_c[:, c, :], xn_t[:, c, :],
                                                start=(c == 0), stop=(c == T - 1))
                    last.then_inc(c_done, 1)
                if past.live:
                    pe.wait_ge(v_copied, held(past.n))
                    for t in range(T):
                        last = nc.tensor.matmul(ps_v[:, t, :], c_t[:, past.slot, t * P:(t + 1) * P], w_v[:, :],
                                                start=True, stop=True)
                    last.then_inc(v_done, 1)

            two = G // 2

            def hi_scores(a, g):
                at = NG * a.n + g
                q = q_st[0:KQ, a.slot, :, :]
                k = k_st[0:KQ, a.slot, :, :]
                if g % 2 == 0:
                    pe.wait_ge(st_in[a.slot][g // 2], PRODUCTS * 16 * a.turn)
                pe.wait_ge(max_hi_done, held(at))
                for b in range(2):
                    for i in range(two):
                        hh = g * G + b * two + i
                        nc.tensor.matmul(ps_hi[:, b * two + i, :], q[:, hh, P:S], k[:, hh, :],
                                         start=(i == 0), stop=False, skip_group_check=True)
                    last = nc.tensor.matmul(ps_hi[:, b * two:(b + 1) * two, P:S], ident_bf[:, :],
                                            mask_qk[:, 0:two, :], start=False, stop=True,
                                            skip_group_check=True)
                last.then_inc(hi_done, 1)

            def lo_scores(a, g):
                q = q_st[0:KQ, a.slot, :, :]
                k = k_st[0:KQ, a.slot, :, :]
                pe.wait_ge(max_lo_done, held(NG * a.n + g))
                for i in range(G):
                    hh = g * G + i
                    nc.tensor.matmul(ps_lo[:, i, :], q[:, hh, 0:P], k[:, hh, 0:P],
                                     start=(i == 0), stop=False, skip_group_check=True)
                nc.tensor.matmul(ps_lo[:, :, :], ident_bf[:, :], mask_qk[:, :, :], start=False, stop=True,
                                 skip_group_check=True).then_inc(lo_done, 1)

            def key_scores(a, g):
                at = NG * a.n + g
                q = q_st[0:KM, a.slot, :, :]
                k = k_st[0:KM, a.slot, :, :]
                if g % 2 == 0:
                    pe.wait_ge(row_in[g // 2], 16 * (a.n + 1))
                pe.wait_ge(exp0_done, held(at))
                for b in range(2):
                    for i in range(two):
                        hh = g * G + b * two + i
                        nc.tensor.matmul(ps_k0[:, b * two + i, :], k[:, hh, 0:P], q[:, hh, :],
                                         start=(i == 0), stop=False, skip_group_check=True)
                    last = nc.tensor.matmul(ps_k0[:, b * two:(b + 1) * two, 0:P], ident_bf[:, :],
                                            mask_kq[:, :, :], start=False, stop=True,
                                            skip_group_check=True)
                last.then_inc(k0_done, 1)
                pe.wait_ge(exp1_done, held(at))
                for i in range(G):
                    hh = g * G + i
                    last = nc.tensor.matmul(ps_k1[:, i, :], k[:, hh, P:S], q[:, hh, P:S],
                                            start=True, stop=True)
                last.then_inc(k1_done, 1)

            def values(a, g):
                at = NG * a.n + g
                if g == 0:
                    pe.wait_ge(v_ready, a.n + 1)
                pe.wait_ge(exp1_done, at + 1)
                pe.wait_ge(o_copied, held(at))
                for i in range(G):
                    nc.tensor.matmul(ps_o[i * VW:(i + 1) * VW, :], v_now[:, a.slot, 0, g * G + i, :],
                                     probs[:, g, i, 0:S], start=True, stop=False, skip_group_check=True)
                for i in range(G):
                    last = nc.tensor.matmul(ps_o[i * VW:(i + 1) * VW, P:S], v_now[:, a.slot, 1, g * G + i, :],
                                            probs[:, g, i, S:S + P], start=False, stop=True,
                                            skip_group_check=True)
                last.then_inc(o_done, 1)

            def turn_max(a, hf):
                pe.wait_ge(cut[3], 2 * a.n + hf + 1)
                pe.wait_ge(mt_copied, held(2 * a.n + hf))
                for t in range(T):
                    last = nc.tensor.transpose(ps_mt[0:PARTS * HALF, t * P:(t + 1) * P],
                                               max_parts[:, t, :, :].rearrange("p c h -> p (c h)"),
                                               ident_bf[:, :])
                last.then_inc(mt_done, 1)

            def turn_output(a, t):
                for g in range(NG):
                    last = nc.tensor.transpose(ps_m[:, g * P:(g + 1) * P],
                                               o_un[:, a.slot, g, t * P:(t + 1) * P], ident[:, :])
                last.then_inc(ot_done, 1)

            def attention(j, u):
                here, done, past = At(j, u, 0), At(j, u, -1), At(j, u, -2)
                for g in range(NG):
                    if here.live:
                        hi_scores(here, g)
                        lo_scores(here, g)
                    if done.live:
                        key_scores(done, g)
                    if g == 0 and done.live:
                        pe.wait_ge(attn_done, held(T * (done.n - 1)))
                        turn_max(done, 1)
                    if g == 2 and here.live:
                        turn_max(here, 0)
                    if g == 3 and past.live:
                        pe.wait_ge(attn_done, T * past.n + 1)
                        turn_output(past, 1)
                    late = done if g >= 2 else past
                    if late.live:
                        values(late, (g - 2) % NG)
                    if g == 2 and past.live:
                        pe.wait_ge(mt_copied, 2 * (past.n + 2) + 1 if here.live else 2 * IMAGES)
                        pe.wait_ge(attn_done, held(T * past.n))
                        pe.wait_ge(o_copied, NG * (past.n + 1))
                        turn_output(past, 0)

            def product(dst, src_t, w, done):
                for t in range(T):
                    for c in range(T):
                        last = nc.tensor.matmul(dst[:, t, :], src_t[:, c, t * P:(t + 1) * P], w[:, c, :],
                                                start=(c == 0), stop=(c == T - 1))
                last.then_inc(done, 1)

            def tail(j, u):
                ahead, here, done = At(j, u, 1), At(j, u, 0), At(j, u, -1)
                if here.live:
                    pe.wait_ge(at_copied, here.n + 1)
                    pe.wait_ge(y_done, held(here.n - 1))
                    product(ps_y[here.slot], a_t, w_out, proj_done)
                if done.live:
                    pe.wait_ge(yn_done, T * (done.n + 1))
                    pe.wait_ge(yt_copied, held(done.n - 1))
                    turn(ps_yt[done.slot], yn, yt_done)
                if ahead.live:
                    pe.wait_ge(a_in[ahead.slot], 16 * ahead.turn)
                    pe.wait_ge(at_copied, held(ahead.n - 1))
                    turn(ps_at[ahead.slot], a_sb[:, ahead.slot, :, :], at_done)
                if done.live:
                    pe.wait_ge(yt_copied, done.n + 1)
                    pe.wait_ge(z_done, held(done.n - 1))
                    if isinstance(done.n, int) and done.n == 0:
                        pe.wait_ge(attn_done, T * IMAGES)
                    product(ps_z[done.slot], yn_t, w_sign, ffn_done)

            pe.wait_ge(drawn, TAPS + 5)
            pe.wait_ge(band_ready, 1)
            pe.wait_ge(compared, 2)
            turn(ps_w, signs, turned)
            pe.wait_ge(up_ready, 1)
            pe.wait_ge(weights_in, 4 * 16)
            steps(pe, front, 0, 2)
            pe.wait_ge(xt_copied, IMAGES)
            pe.wait_ge(abs_done, T * IMAGES)
            pe.wait_ge(c_copied, IMAGES)
            pe.wait_ge(ones_set, 1)
            pe.wait_ge(rest_done, IMAGES)
            pe.wait_ge(v_copied, IMAGES)
            pe.wait_ge(sign_ready, 1)
            steps(pe, attention, 0, 2)
            pe.wait_ge(max_lo_done, NG * IMAGES)
            pe.wait_ge(exp1_done, NG * IMAGES)
            pe.wait_ge(o_copied, NG * IMAGES)
            steps(pe, tail, 1, 1)


_INS = ['x', 'L0_tok_scharr', 'L0_attn_W_dq', 'L0_attn_W_uq', 'L0_attn_W_dkv', 'L0_attn_W_uk',
        'L0_attn_W_uv', 'L0_attn_W_o', 'L0_ffn_weight']


def kernel(**inputs):
    import numpy as _np
    import concourse.bacc as _bacc
    from concourse import mybir as _mybir
    from concourse.bass_utils import run_bass_kernel_spmd as _run

    nc = _bacc.Bacc("TRN2", target_bir_lowering=False, num_devices=1)
    arrays, args = {}, []
    for name in _INS:
        a = _np.ascontiguousarray(inputs[name])
        arrays[f"in_{name}"] = a
        args.append(nc.dram_tensor(f"in_{name}", a.shape, _mybir.dt.from_np(a.dtype), kind="ExternalInput").ap())
    out = nc.dram_tensor("out_dram", (IMAGES, S, D), F32, kind="ExternalOutput").ap()
    build(nc, *args, out)
    r = _run(nc, [arrays], core_ids=[0])
    return r.results[0]["out_dram"]
```
